# Optimizing a Trainium2 kernel written in Bass

```python
import numpy as np
import jax
import jax.numpy as jnp

def _softmax(x, axis=-1):
    return jax.nn.softmax(x, axis=axis)

def _gelu(x):
    return jax.nn.gelu(x, approximate=True)

def _silu(x):
    return jax.nn.silu(x)

def _sigmoid(x):
    return jax.nn.sigmoid(x)

def _layernorm(x, axis=-1, eps=1e-05):
    m = jnp.mean(x, axis=axis, keepdims=True)
    v = jnp.var(x, axis=axis, keepdims=True)
    return (x - m) / jnp.sqrt(v + eps)

def _scatter_add(tgt, idx, src, axis=0):
    return tgt.at[idx].add(src)

def _segment_sum(src, seg, n):
    return jax.ops.segment_sum(src, seg, n)
kernel_name = 'mk_conv_preact_d2_conv_nchw256_r2_8e9379'

def setup_inputs(seed: int=0):
    np.random.seed(seed)
    _w = jnp.asarray

    def _rec_inputs():
        import jax
        import jax.numpy as jnp
        _gk = jax.random.key(seed)
        x = -0.0003929 + 0.9999 * jax.random.normal(jax.random.fold_in(_gk, 1), (16, 128, 32, 32), jnp.float32)
        return x
    x = _rec_inputs()

    def _L0_conv_setup():
        import jax, jax.numpy as jnp
        import numpy as np
        E = 8
        K = 2
        G = 8
        TEMP = 1.0
        EPS = 1e-05
        B, CIN, COUT, H, W = (16, 128, 128, 32, 32)

        def _conv(x, w, groups, padding):
            return jax.lax.conv_general_dilated(x, w, window_strides=(1, 1), padding=padding, dimension_numbers=('NCHW', 'OIHW', 'NCHW'), feature_group_count=groups)

        def _group_norm(x, gamma, beta):
            b, c, h, w = x.shape
            xg = x.reshape(b, G, c // G, h, w)
            m = xg.mean(axis=(2, 3, 4), keepdims=True)
            v = xg.var(axis=(2, 3, 4), keepdims=True)
            xn = ((xg - m) * jax.lax.rsqrt(v + EPS)).reshape(b, c, h, w)
            return xn * gamma[:, None, None] + beta[:, None, None]
        key = jax.random.key(seed)
        ks = jax.random.split(key, 4)
        x = jax.random.normal(ks[0], (B, CIN, H, W), dtype=jnp.float32)
        router_w = jax.random.normal(ks[1], (E, 2 * CIN), dtype=jnp.float32) * 0.01
        fused_w = jax.random.normal(ks[2], (E * COUT, CIN // G, 3, 3), dtype=jnp.float32) * float(np.sqrt(2.0 / (E * COUT * 9)))
        shared_w = jax.random.normal(ks[3], (COUT, CIN // G, 1, 1), dtype=jnp.float32) * float(np.sqrt(2.0 / COUT))
        gn_shared_g = jnp.ones((COUT,), jnp.float32)
        gn_shared_b = jnp.zeros((COUT,), jnp.float32)
        expert_g = jnp.ones((E, COUT), jnp.float32)
        expert_b = jnp.zeros((E, COUT), jnp.float32)
        return {'x': x, 'router_w': router_w, 'fused_w': fused_w, 'shared_w': shared_w, 'gn_shared_g': gn_shared_g, 'gn_shared_b': gn_shared_b, 'expert_g': expert_g, 'expert_b': expert_b}
    _L0_conv_all = _L0_conv_setup()
    _L0_conv_in = {k: v for k, v in _L0_conv_all.items() if k in ('router_w', 'fused_w', 'shared_w', 'gn_shared_g', 'gn_shared_b', 'expert_g', 'expert_b')}
    del _L0_conv_all

    def _L1_conv_setup():
        import jax, jax.numpy as jnp
        import numpy as np
        DIM = 128
        HEADS = 8
        HD = DIM // HEADS
        WS = 8
        N = WS * WS
        BN_SCALE = 1.0 / np.sqrt(1.0 + 1e-05)

        def _relative_position_index():
            coords = np.stack(np.meshgrid(np.arange(WS), np.arange(WS), indexing='ij'))
            cf = coords.reshape(2, -1)
            rel = cf[:, :, None] - cf[:, None, :]
            rel = rel.transpose(1, 2, 0)
            rel[:, :, 0] += WS - 1
            rel[:, :, 1] += WS - 1
            rel[:, :, 0] *= 2 * WS - 1
            return jnp.asarray(rel.sum(-1))

        def _relative_coords_table():
            r = np.arange(-(WS - 1), WS, dtype=np.float32)
            g = np.stack(np.meshgrid(r, r, indexing='ij'), axis=-1)
            g = g / (WS - 1) * 8.0
            g = np.sign(g) * np.log2(np.abs(g) + 1.0) / np.log2(8.0)
            return jnp.asarray(g)
        key = jax.random.key(seed)
        ks = jax.random.split(key, 9)
        B, H, W = (16, 32, 32)
        s = 0.02
        return {'x': jax.random.normal(ks[0], (B, DIM, H, W), dtype=jnp.float32), 'qkv_w': jax.random.normal(ks[1], (3 * DIM, DIM), dtype=jnp.float32) * s, 'qkv_b': jax.random.normal(ks[2], (3 * DIM,), dtype=jnp.float32) * s, 'proj_w': jax.random.normal(ks[3], (DIM, DIM), dtype=jnp.float32) * s, 'proj_b': jax.random.normal(ks[4], (DIM,), dtype=jnp.float32) * s, 'cpb_w1': jax.random.normal(ks[5], (DIM, 2), dtype=jnp.float32) * 0.5, 'cpb_b1': jax.random.normal(ks[6], (DIM,), dtype=jnp.float32) * 0.5, 'cpb_w2': jax.random.normal(ks[7], (HEADS, DIM), dtype=jnp.float32) * 0.1, 'dw_w': jax.random.normal(ks[8], (DIM, 1, 7, 7), dtype=jnp.float32) * s}
    _L1_conv_all = _L1_conv_setup()
    _L1_conv_in = {k: v for k, v in _L1_conv_all.items() if k in ('qkv_w', 'qkv_b', 'proj_w', 'proj_b', 'cpb_w1', 'cpb_b1', 'cpb_w2', 'dw_w')}
    del _L1_conv_all
    return {'x': x, 'L0_conv_router_w': _L0_conv_in['router_w'], 'L0_conv_fused_w': _L0_conv_in['fused_w'], 'L0_conv_shared_w': _L0_conv_in['shared_w'], 'L0_conv_gn_shared_g': _L0_conv_in['gn_shared_g'], 'L0_conv_gn_shared_b': _L0_conv_in['gn_shared_b'], 'L0_conv_expert_g': _L0_conv_in['expert_g'], 'L0_conv_expert_b': _L0_conv_in['expert_b'], 'L1_conv_qkv_w': _L1_conv_in['qkv_w'], 'L1_conv_qkv_b': _L1_conv_in['qkv_b'], 'L1_conv_proj_w': _L1_conv_in['proj_w'], 'L1_conv_proj_b': _L1_conv_in['proj_b'], 'L1_conv_cpb_w1': _L1_conv_in['cpb_w1'], 'L1_conv_cpb_b1': _L1_conv_in['cpb_b1'], 'L1_conv_cpb_w2': _L1_conv_in['cpb_w2'], 'L1_conv_dw_w': _L1_conv_in['dw_w']}

def reference(x, L0_conv_router_w, L0_conv_fused_w, L0_conv_shared_w, L0_conv_gn_shared_g, L0_conv_gn_shared_b, L0_conv_expert_g, L0_conv_expert_b, L1_conv_qkv_w, L1_conv_qkv_b, L1_conv_proj_w, L1_conv_proj_b, L1_conv_cpb_w1, L1_conv_cpb_b1, L1_conv_cpb_w2, L1_conv_dw_w):
    import jax
    import jax.numpy as jnp

    def _L0_conv_ref(x, router_w, fused_w, shared_w, gn_shared_g, gn_shared_b, expert_g, expert_b):
        import jax, jax.numpy as jnp
        import numpy as np
        E = 8
        K = 2
        G = 8
        TEMP = 1.0
        EPS = 1e-05
        B, CIN, COUT, H, W = (16, 128, 128, 32, 32)

        def _conv(x, w, groups, padding):
            return jax.lax.conv_general_dilated(x, w, window_strides=(1, 1), padding=padding, dimension_numbers=('NCHW', 'OIHW', 'NCHW'), feature_group_count=groups)

        def _group_norm(x, gamma, beta):
            b, c, h, w = x.shape
            xg = x.reshape(b, G, c // G, h, w)
            m = xg.mean(axis=(2, 3, 4), keepdims=True)
            v = xg.var(axis=(2, 3, 4), keepdims=True)
            xn = ((xg - m) * jax.lax.rsqrt(v + EPS)).reshape(b, c, h, w)
            return xn * gamma[:, None, None] + beta[:, None, None]
        b = x.shape[0]
        mean = x.mean(axis=(2, 3))
        std = x.std(axis=(2, 3), ddof=1)
        stats = jnp.concatenate([mean, std], axis=1)
        p1 = jax.nn.softmax(stats @ router_w.T, axis=1)
        logits = jnp.clip(p1 / TEMP, -30.0, 30.0)
        probs = jax.nn.softmax(logits, axis=1)
        topk_p, topk_i = jax.lax.top_k(probs, K)
        rw = topk_p / (topk_p.sum(axis=1, keepdims=True) + 1e-06)
        shared = _conv(x, shared_w, G, 'VALID')
        shared = jax.nn.silu(_group_norm(shared, gn_shared_g, gn_shared_b))
        fused = _conv(x, fused_w, G, 'SAME').reshape(b, E, COUT, H, W)
        eo = jnp.take_along_axis(fused, topk_i[:, :, None, None, None], axis=1)
        eg = eo.reshape(b, K, G, COUT // G, H, W)
        m = eg.mean(axis=(3, 4, 5), keepdims=True)
        v = eg.var(axis=(3, 4, 5), keepdims=True)
        en = ((eg - m) * jax.lax.rsqrt(v + EPS)).reshape(b, K, COUT, H, W)
        gam = expert_g[topk_i]
        bet = expert_b[topk_i]
        en = en * gam[..., None, None] + bet[..., None, None]
        expert_out = (jax.nn.silu(en) * rw[:, :, None, None, None]).sum(axis=1)
        return shared + expert_out

    def _L1_conv_ref(x, qkv_w, qkv_b, proj_w, proj_b, cpb_w1, cpb_b1, cpb_w2, dw_w):
        import jax, jax.numpy as jnp
        import numpy as np
        DIM = 128
        HEADS = 8
        HD = DIM // HEADS
        WS = 8
        N = WS * WS
        BN_SCALE = 1.0 / np.sqrt(1.0 + 1e-05)

        def _relative_position_index():
            coords = np.stack(np.meshgrid(np.arange(WS), np.arange(WS), indexing='ij'))
            cf = coords.reshape(2, -1)
            rel = cf[:, :, None] - cf[:, None, :]
            rel = rel.transpose(1, 2, 0)
            rel[:, :, 0] += WS - 1
            rel[:, :, 1] += WS - 1
            rel[:, :, 0] *= 2 * WS - 1
            return jnp.asarray(rel.sum(-1))

        def _relative_coords_table():
            r = np.arange(-(WS - 1), WS, dtype=np.float32)
            g = np.stack(np.meshgrid(r, r, indexing='ij'), axis=-1)
            g = g / (WS - 1) * 8.0
            g = np.sign(g) * np.log2(np.abs(g) + 1.0) / np.log2(8.0)
            return jnp.asarray(g)
        B, C, H, W = x.shape
        Hn, Wn = (H // WS, W // WS)
        B_ = B * Hn * Wn
        tbl = _relative_coords_table()
        h = jax.nn.silu((tbl @ cpb_w1.T + cpb_b1) * BN_SCALE)
        bias_table = h @ cpb_w2.T * BN_SCALE
        bias_table = bias_table.reshape(-1, HEADS)
        rpi = _relative_position_index()
        bias = bias_table[rpi.reshape(-1)].reshape(N, N, HEADS).transpose(2, 0, 1)
        bias = 16.0 * jax.nn.sigmoid(bias)
        qkv = jnp.einsum('oc,bchw->bohw', qkv_w, x) + qkv_b[None, :, None, None]
        win = qkv.reshape(B, 3 * C, Hn, WS, Wn, WS).transpose(0, 2, 4, 1, 3, 5)
        win = win.reshape(B_, 3 * C, N)
        qkvw = win.reshape(B_, 3, HEADS, HD, N).transpose(1, 0, 2, 4, 3)
        q, k, v = (qkvw[0], qkvw[1], qkvw[2])
        scores = jnp.einsum('bhnd,bhmd->bhnm', q, k) / np.sqrt(HD) + bias[None]
        attn = jax.nn.softmax(scores, axis=-1)
        o = jnp.einsum('bhnm,bhmd->bhnd', attn, v)

        def window_reverse(w):
            t = w.reshape(B, Hn, Wn, WS, WS, C).transpose(0, 5, 1, 3, 2, 4)
            return t.reshape(B, C, H, W)
        x_img = window_reverse(o.transpose(0, 2, 1, 3).reshape(B_, N, C))
        v_img = window_reverse(v.transpose(0, 2, 1, 3).reshape(B_, N, C))
        pe = jax.lax.conv_general_dilated(v_img, dw_w, window_strides=(1, 1), padding='SAME', feature_group_count=C, dimension_numbers=('NCHW', 'OIHW', 'NCHW'))
        out = x_img + pe
        out = jnp.einsum('oc,bchw->bohw', proj_w, out) + proj_b[None, :, None, None]
        return out

    def _gn(v, G=32, eps=1e-05):
        B_, C_, H_, W_ = v.shape
        g = v.reshape(B_, G, C_ // G, H_, W_)
        m = jnp.mean(g, axis=(2, 3, 4), keepdims=True)
        s = jnp.var(g, axis=(2, 3, 4), keepdims=True)
        return ((g - m) / jnp.sqrt(s + eps)).reshape(v.shape)

    def _ln_c(v, eps=1e-06):
        m = jnp.mean(v, axis=1, keepdims=True)
        s = jnp.var(v, axis=1, keepdims=True)
        return (v - m) / jnp.sqrt(s + eps)

    def _ln_t(v, eps=1e-05):
        m = jnp.mean(v, axis=-1, keepdims=True)
        s = jnp.var(v, axis=-1, keepdims=True)
        return (v - m) / jnp.sqrt(s + eps)

    def _to_tokens(v):
        B_, C_, H_, W_ = v.shape
        return v.reshape(B_, C_, H_ * W_).transpose(0, 2, 1)

    def _from_tokens(t, like):
        B_, C_, H_, W_ = like.shape
        return t.transpose(0, 2, 1).reshape(B_, C_, H_, W_)
    x = x + _L0_conv_ref(_gn(x), L0_conv_router_w, L0_conv_fused_w, L0_conv_shared_w, L0_conv_gn_shared_g, L0_conv_gn_shared_b, L0_conv_expert_g, L0_conv_expert_b)
    x = x + _L1_conv_ref(_gn(x), L1_conv_qkv_w, L1_conv_qkv_b, L1_conv_proj_w, L1_conv_proj_b, L1_conv_cpb_w1, L1_conv_cpb_b1, L1_conv_cpb_w2, L1_conv_dw_w)
    return x

_drawn_inputs = setup_inputs


def setup_inputs(seed=0):
    import zlib

    import numpy as np

    out = dict(_drawn_inputs(seed))
    spreads = {'L0_conv_gn_shared_g': (1.0, 0.2),
     'L0_conv_gn_shared_b': (0.0, 0.1),
     'L0_conv_expert_g': (1.0, 0.2),
     'L0_conv_expert_b': (0.0, 0.1)}
    factors = {'L1_conv_qkv_w': 6.132,
     'L1_conv_qkv_b': 8.0,
     'L1_conv_proj_w': 5.831,
     'L1_conv_proj_b': 3.606,
     'L1_conv_cpb_w1': 8.0,
     'L1_conv_cpb_b1': 8.0,
     'L1_conv_cpb_w2': 8.0,
     'L1_conv_dw_w': 8.0}
    for name, (base, spread) in spreads.items():
        noise = np.random.default_rng([zlib.crc32(name.encode()), seed]).standard_normal(out[name].shape)
        drawn = base * np.exp(spread * noise) if base else spread * noise
        out[name] = jnp.asarray(drawn.astype(out[name].dtype))
    for name, factor in factors.items():
        out[name] = (out[name] * factor).astype(out[name].dtype)
    return out
```

```python
from contextlib import ExitStack

import concourse.bass as bass
from concourse import mybir

F32 = mybir.dt.float32
F16 = mybir.dt.float16
BF16 = mybir.dt.bfloat16
I32 = mybir.dt.int32
U32 = mybir.dt.uint32
ALU = mybir.AluOpType
ACT = mybir.ActivationFunctionType
AX = mybir.AxisListType

B, C, H, W = 16, 128, 32, 32
PIX = H * W
HALF = PIX // 2
E = 8
TOP = 2
QD = 32
Q = C // QD
HEADS, HD = 8, 16
WS = 8
TOK = WS * WS
ROWS = H // WS
WROW = PIX // ROWS
PAIRS = (PIX // TOK) // 2
PAD = 3
HP = H + 2 * PAD
DWK = 7
HANK = 64
SLOT = B * HP
EPS = 1e-5
BN = float(1.0 / (1.0 + 1e-5) ** 0.5)
REL = 2 * WS - 1
GC = C // E
SH = 2 * 3 * GC
WPAD = W + 2
RUN = H * WPAD + W

WQ, WK, WV, WP, WSH = (C * n for n in range(5))
RWM = 5 * C
RWS = RWM + E
CW2 = RWS + E
EXG = CW2 + HEADS
EXB = EXG + E
VEC = EXB + E
SHG, SHB, BQ, BK, BV, BP = range(VEC, VEC + 6)
WCOLS = VEC + 6
AV4, AV16, OM = 0, C, 2 * C
PM = 2 * C + QD
CCOLS = PM + 2
ID, ID2, SEL, EYE, ONE, TBL = 0, C, 2 * C, 2 * C + 4 * C, 2 * C + 4 * C + B, 2 * C + 4 * C + B + C
TABLE = WS * REL * WS
TCOLS = TBL + TABLE

G_CONV, G_QKV, G_IMAGE = 6, 8, 16
SM_SETUP, SM_IMAGE = 4, PAIRS + 2

SEMS = """
w_loaded x_loaded0 x_loaded1 x_loaded2 x_loaded3
setup_dve setup_act setup_pe setup_pool
xin_loaded xn_saved rows_loaded xn_done chosen chosen_w g_ready
y_copied bn_done aggr_done squares_done sums_done sm_ready setup_read group_read group_square group_var
rstd_done coef_scale coef_shift coefs_done silu_done sum_shared sum_first xr_done
xw_done x1_copied q_hi k_hi q_lo k_lo q_saved k_split k_saved q_stacked k_stacked
v_done v_turned vt_done vp_done s_ready s_max mx_done c_hi c_lo ct_done st_ready exp_done pv_done
recip_done o_done acc_done acc_saved vt_clear
tap_zero tap_loaded0 tap_loaded1 tap_loaded2 tap_loaded3 dw_ready dw_copied pe_turned acc_loaded out_done stored settled_sp settled_pool settled_dve
""".split()


def program(nc, x, wa, wx, dw, l1, cst, tmp, out):
    with ExitStack() as ctx:
        def sb(name, shape, dt=F32):
            return ctx.enter_context(nc.sbuf_tensor(name, shape, dt))

        def bank(name):
            return ctx.enter_context(nc.psum_tensor(name, [C, 512], F32))

        vt = sb("vt", [C, QD * SLOT])
        vt4 = vt[:, :].rearrange("p (c b y) -> p c b y", c=QD, b=B)
        xall = vt[:, 0:B * PIX].rearrange("p (b n) -> p b n", b=B)
        xsh = sb("xsh", [SH, TOP, H + 1, WPAD])
        y = sb("y", [C, 3, PIX])
        tc = y[:, :, :].rearrange("p k n -> p (k n)")
        xin = sb("xin", [C, PIX])
        xn = sb("xn", [C, H + 2, WPAD])
        xr = sb("xr", [C, PIX])
        x1 = sb("x1", [C, PIX])
        xw = sb("xw", [C, PIX])
        vn = sb("vn", [C, PIX])
        vtmp = sb("vtmp", [C, PIX])
        o = sb("o", [C, PIX])
        qhl = sb("qhl", [C, 2, PIX], F16)
        khl = sb("khl", [C, 2, PIX], F16)
        kpar = sb("kpar", [C, 2, 2 * PAIRS, 2, TOK], F16)
        stack = sb("stack", [C, 3 * Q * PIX // 2])
        qs = stack[:, 0:Q * PIX // 2].bitcast(F16).rearrange("p (i n) -> p i n", i=Q)
        ks = stack[:, Q * PIX // 2:].bitcast(F16).rearrange("p (i n) -> p i n", i=Q)
        taps = stack[:, 0:4 * DWK * C].rearrange("p (s d m) -> p s d m", s=4, d=DWK)
        pt = sb("pt", [C, 2, 2, Q, TOK])
        vp = sb("vp", [C, 2 * PAIRS, Q, QD])
        wsel = sb("wsel", [SH, TOP, 2 * C])
        w = sb("w", [C, WCOLS])
        cc = sb("cc", [C, CCOLS])
        bias = sb("bias", [C, Q * C], F16)
        sel = sb("sel", [2 * HEADS, Q * C], BF16)
        ident2 = sb("ident2", [C, C], F16)
        identb = sb("identb", [C, C], BF16)
        rec = sb("rec", [C, WROW])
        gn0 = sb("gn0", [C, 2, B])
        route = sb("route", [C, B, 4])
        rnum = sb("rnum", [1, B * 4], I32)
        st = sb("st", [C, 6, 6])
        mv = sb("mv", [C, 3, 2])
        sq = sb("sq", [C, 3])
        gs = sb("gs", [C, 3, 2])
        var = sb("var", [C, 3])
        rstd = sb("rstd", [C, 3])
        power = sb("power", [C, 2, 2 * B])
        gb = sb("gb", [C, 2, 3])
        coef = sb("coef", [C, 2, 3])
        shift = sb("shift", [C, 3])
        coef2 = sb("coef2", [C, 2])
        mx = sb("mx", [C, HEADS])
        cm = sb("cm", [C, 2 * HEADS], BF16)
        ct = sb("ct", [2 * HEADS, C], BF16)
        btot = sb("btot", [C, 1])
        sst = sb("sst", [C, 2 * B, 6])
        smv = sb("smv", [C, B, 2])
        ssq = sb("ssq", [C, B])
        sva = sb("sva", [C, B])
        sgs = sb("sgs", [C, B, 2])
        srs = sb("srs", [C, 2 * B])
        rs = sb("rs", [B, 64])
        rb = sb("rb", [B, B, 4])
        ri = sb("ri", [B, 8], U32)
        l1s = sb("l1s", [3, C])
        hb = o[:, 0:TABLE]

        g = [bank("g0"), bank("g1")]
        sbk = [bank("s0"), bank("s1")]
        tbk = [bank("t0"), bank("t1")]
        pvb = bank("pv")
        sm = bank("sm")
        smb = sm[:, :].bitcast(BF16)

        xs = nc.dram_tensor("xs", [C, (H + 2) * WPAD], F32).ap()
        sq_d = nc.dram_tensor("sq_d", [2, C, PIX], F16).ap()
        sk_d = nc.dram_tensor("sk_d", [2, C, 2 * PIX], F16).ap()
        acc_d = nc.dram_tensor("acc_d", [B, C, PIX], F32).ap()

        sem = {n: ctx.enter_context(nc.semaphore(n)) for n in SEMS}
        tap_loaded = [sem[f"tap_loaded{n}"] for n in range(4)]
        x_loaded = [sem[f"x_loaded{n}"] for n in range(4)]

        def conv_use(j):
            return 0 if isinstance(j, int) and j == 0 else G_IMAGE * j + G_CONV - G_IMAGE + G_QKV

        def qkv_use(b):
            return G_IMAGE * b + G_CONV

        def proj_use(b):
            last = isinstance(b, int) and b == B - 1
            return G_IMAGE * b + G_CONV + (G_QKV if last else G_QKV + G_CONV)

        LAST_USE = proj_use(B - 1) + 2

        def sm_use(b, n):
            return SM_SETUP + 3 + SM_IMAGE * b + n

        def small_slots(b):
            if isinstance(b, int) and b == B - 1:
                return {f"max{p}": p for p in range(PAIRS)}
            names = ["max0", "gn_y"] + [f"max{p}" for p in range(1, 6)] + ["gn_x", "max6", "max7"]
            return {n: k for k, n in enumerate(names)}

        def images(eng, step):
            step(0, True, True)
            with eng.Fori(1, B - 2) as b:
                step(b, True, True)
            step(B - 2, True, False)
            step(B - 1, False, False)

        block = ctx.enter_context(nc.Block())

        @block.sync
        def _(sp):
            xb = x.rearrange("b c h w -> c b (h w)")
            sp.dma_start(w[:, :], wa).then_inc(sem["w_loaded"], 16)
            sp.dma_start(cc[:, :], cst).then_inc(sem["w_loaded"], 16)
            sp.dma_start(tc[:, 0:TCOLS], tmp).then_inc(sem["w_loaded"], 16)
            sp.dma_start(l1s[:, :], l1).then_inc(sem["w_loaded"], 16)
            for n in range(4):
                sp.dma_start(xall[:, 4 * n:4 * n + 4, :], xb[:, 4 * n:4 * n + 4, :]).then_inc(x_loaded[n], 16)

            def load_x(j):
                if not (isinstance(j, int) and j == 0):
                    sp.wait_ge(sem["xr_done"], j)
                    sp.sem_inc(sem["settled_sp"], 1)
                src = x[j] if isinstance(j, int) else x[bass.ds(j, 1)]
                src = src.rearrange("c h w -> c (h w)") if isinstance(j, int) else src.rearrange("b c h w -> c (b h w)")
                sp.dma_start(xin[:, :], src).then_inc(sem["xin_loaded"], 16)

            def save_xn(j):
                sp.wait_ge(sem["xn_done"], j + 1)
                sp.sem_inc(sem["settled_sp"], 1)
                if not (isinstance(j, int) and j == 0):
                    sp.wait_ge(sem["rows_loaded"], 32 * TOP * j)
                    sp.sem_inc(sem["settled_sp"], 1)
                sp.dma_start(xs, xn[:, :, :].rearrange("p h w -> p (h w)")).then_inc(sem["xn_saved"], 16)

            def stack_qk(b):
                sp.wait_ge(sem["q_lo"], 2 * b + 2)
                sp.sem_inc(sem["settled_sp"], 1)
                sp.dma_start(sq_d.rearrange("t c n -> c t n"), qhl[:, :, :]).then_inc(sem["q_saved"], 16)
                sp.wait_ge(sem["k_split"], b + 1)
                sp.sem_inc(sem["settled_sp"], 1)
                sp.dma_start(sk_d.rearrange("t c n -> c t n"),
                             kpar[:, :, :, :, :].rearrange("p t w a m -> p t (w a m)")).then_inc(sem["k_saved"], 16)
                sp.wait_ge(sem["q_saved"], 16 * b + 16)
                sp.sem_inc(sem["settled_sp"], 1)
                sp.wait_ge(sem["st_ready"], PAIRS * b)
                sp.sem_inc(sem["settled_sp"], 1)
                for part, t in enumerate((0, 1, 0)):
                    sp.dma_start(qs[QD * part:QD * part + QD, :, :],
                                 sq_d[t].rearrange("(i c) n -> c i n", i=Q)).then_inc(sem["q_stacked"], 16)
                sp.wait_ge(sem["k_saved"], 16 * b + 16)
                sp.sem_inc(sem["settled_sp"], 1)
                for part, t in enumerate((0, 0, 1)):
                    sp.dma_start(ks[QD * part:QD * part + QD, :, :],
                                 sk_d[t].rearrange("(i c) n -> c i n", i=Q)).then_inc(sem["k_stacked"], 16)

            def save_acc(b):
                sp.wait_ge(sem["acc_done"], 2 * b + 2)
                sp.sem_inc(sem["settled_sp"], 1)
                dst = (acc_d[b] if isinstance(b, int)
                       else acc_d[bass.ds(b, 1)].rearrange("b c n -> c (b n)"))
                sp.dma_start(dst, x1[:, :]).then_inc(sem["acc_saved"], 16)

            def step(b, has1, has2):
                stack_qk(b)
                if has2:
                    load_x(b + 2)
                    save_xn(b + 2)
                save_acc(b)

            load_x(0)
            save_xn(0)
            load_x(1)
            save_xn(1)
            images(sp, step)

            def load_taps(c, s):
                for q in range(Q):
                    at = (QD * q + c) * DWK * HANK
                    sp.dma_start(taps[QD * q:QD * q + QD, s, :, QD * q:QD * q + QD],
                                 bass.AP(dw.tensor, at, [[1, QD], [HANK, DWK], [1, QD]])).then_inc(tap_loaded[s], 16)

            sp.wait_ge(sem["tap_zero"], 1)
            for c in range(QD):
                if c >= 4:
                    sp.wait_ge(sem["dw_ready"], c - 3)
                load_taps(c, c % 4)

            def load_acc(b):
                buf = (xin, xw)[b % 2]
                sp.dma_start(buf[:, :], acc_d[b]).then_inc(sem["acc_loaded"], 16)

            sp.wait_ge(sem["acc_saved"], 16 * B)
            load_acc(0)
            load_acc(1)
            for b in range(B):
                sp.wait_ge(sem["out_done"], 2 * b + 2)
                sp.dma_start(out[b].rearrange("c h w -> c (h w)"), (xr, x1)[b % 2][:, :]).then_inc(sem["stored"], 16)
                if b + 2 < B:
                    sp.wait_ge(sem["acc_loaded"], 16 * (b + 2))
                    load_acc(b + 2)
            sp.wait_ge(sem["stored"], 16 * B)

        @block.gpsimd
        def _(pool):
            pool.memset(power[:, 0, :], -0.5)
            pool.memset(power[:, 1, :], 0.5)
            pool.memset(xn[:, :, :], 0.0)
            pool.memset(vp[:, :, :, :], 0.0).then_inc(sem["setup_pool"], 1)
            pool.wait_ge(sem["setup_pool"], 1)
            pool.wait_ge(sem["setup_dve"], 8)
            nc.gpsimd.tensor_tensor(srs[:, 0:B], sva[:, :], power[:, 0, 0:B], ALU.pow)
            nc.gpsimd.tensor_tensor(srs[:, B:2 * B], ssq[:, :], power[:, 1, 0:B], ALU.pow).then_inc(sem["setup_pool"], 1)
            pool.wait_ge(sem["setup_dve"], 3)
            rows = vt[:, :].rearrange("p (s y) -> p s y", y=HP)
            pool.memset(rows[:, :, 0:PAD], 0.0)
            pool.memset(rows[:, :, HP - PAD:HP], 0.0).then_inc(sem["vt_clear"], 1)

            def choose(j):
                if isinstance(j, int) and j == 0:
                    pool.wait_ge(sem["setup_dve"], 31)
                    pool.wait_ge(sem["setup_pool"], 2)
                else:
                    pool.wait_ge(sem["g_ready"], conv_use(j - 1) + G_CONV)
                    pool.wait_ge(sem["coefs_done"], j)
                pool.sem_inc(sem["settled_pool"], 1)
                nc.gpsimd.tensor_copy(gb[:, 0, 0:1], w[:, SHG:SHG + 1])
                nc.gpsimd.tensor_copy(gb[:, 1, 0:1], w[:, SHB:SHB + 1])
                for k in range(TOP):
                    e = pool.value_load(rnum[0:1, bass.ds(4 * j + 2 + k, 1)], min_val=0, max_val=E - 1)
                    pool.dma_start(wsel[:, k, :], wx[bass.ds(e, 1)].rearrange("e p n -> p (e n)")
                                   ).then_inc(sem["chosen_w"], 16)
                    nc.gpsimd.tensor_copy(gb[:, 0, 1 + k:2 + k], w[:, bass.ds(e + EXG, 1)])
                    last = nc.gpsimd.tensor_copy(gb[:, 1, 1 + k:2 + k], w[:, bass.ds(e + EXB, 1)])
                last.then_inc(sem["chosen"], 1)

            def load_rows(j):
                pool.wait_ge(sem["xn_saved"], 16 * j + 16)
                pool.sem_inc(sem["settled_pool"], 1)
                for k in range(TOP):
                    e = pool.value_load(rnum[0:1, bass.ds(4 * j + 2 + k, 1)], min_val=0, max_val=E - 1)
                    size = (H + 2) * WPAD
                    for s in range(2):
                        src = bass.AP(xs.tensor, e * (GC * size) + s * WPAD, [[1, 3], [size, GC], [1, RUN]])
                        dst = xsh[SH // 2 * s:SH // 2 * (s + 1), k, :, :].rearrange("p h w -> p (h w)")[:, 0:RUN]
                        pool.dma_start(dst, src).then_inc(sem["rows_loaded"], 16)

            def rsqrt(j, n, count):
                pool.wait_ge(sem["group_var"], 2 * j + n + 1)
                nc.gpsimd.tensor_tensor(rstd[:, 0:count], var[:, 0:count], power[:, 0, 0:count],
                                        ALU.pow).then_inc(sem["rstd_done"], 1)

            def step(b, has1, has2):
                pool.wait_ge(sem["xr_done"], b + 1)
                pool.wait_ge(sem["acc_saved"], 16 * b)
                pool.sem_inc(sem["settled_pool"], 1)
                nc.gpsimd.tensor_copy(x1[:, :], xr[:, :]).then_inc(sem["x1_copied"], 1)
                pool.wait_ge(sem["v_turned"], b + 1)
                pool.sem_inc(sem["settled_pool"], 1)
                src = vtmp[:, :].rearrange("p (c y) -> p c y", c=QD)
                dst = vt[:, :].rearrange("p (c s) -> p c s", c=QD)[:, :, bass.ds(b * HP + PAD, H)]
                nc.gpsimd.tensor_copy(dst, src).then_inc(sem["vt_done"], 1)
                if has1:
                    rsqrt(b + 1, 0, 3)
                if has2:
                    choose(b + 2)
                if has1:
                    rsqrt(b + 1, 1, 1)
                if has2:
                    load_rows(b + 2)

            choose(0)
            load_rows(0)
            rsqrt(0, 0, 3)
            choose(1)
            rsqrt(0, 1, 1)
            load_rows(1)
            pool.wait_ge(sem["vt_clear"], 1)
            images(pool, step)

            pool.wait_ge(sem["st_ready"], B * PAIRS)
            pool.memset(stack[:, 0:4 * DWK * C], 0.0).then_inc(sem["tap_zero"], 1)

        @block.scalar
        def _(act):
            act.wait_ge(sem["setup_pe"], 1)
            act.activation(hb[:, 0:TABLE // 2], tbk[0][:, 0:TABLE // 2], ACT.Silu, scale=BN)
            act.activation(hb[:, TABLE // 2:], sbk[0][:, 0:TABLE // 2], ACT.Silu, scale=BN).then_inc(sem["setup_act"], 1)
            act.wait_ge(sem["setup_pe"], 2)
            act.activation(xw[:, 0:512], tbk[1][:, :], ACT.Sigmoid, scale=BN).then_inc(sem["setup_act"], 1)
            for n in range(2):
                act.wait_ge(sem["setup_dve"], (14, 19)[n])
                act.activation(rs[:, 8:16], rs[:, 0:8], ACT.Exp, bias=rs[:, 16:17],
                               accum_out=rs[:, 17:18]).then_inc(sem["setup_act"], 1)

            def normalise(j):
                act.wait_ge(sem["xin_loaded"], 16 * j + 16)
                if isinstance(j, int) and j == 0:
                    act.wait_ge(sem["setup_dve"], 9)
                    act.wait_ge(sem["setup_pool"], 1)
                    sc, sh = gn0[:, 0, 0:1], gn0[:, 1, 0:1]
                else:
                    act.wait_ge(sem["xn_saved"], 16 * j)
                    act.wait_ge(sem["g_ready"], conv_use(j - 1) + G_CONV)
                    sc, sh = gn0[:, 0, bass.ds(j, 1)], gn0[:, 1, bass.ds(j, 1)]
                act.activation(xn[:, 1:H + 1, 1:W + 1], xin[:, :].rearrange("p (y x) -> p y x", x=W), ACT.Identity, bias=sh, scale=sc).then_inc(sem["xn_done"], 1)

            def copy_y(j):
                u = conv_use(j)
                if isinstance(j, int) and j == 0:
                    act.wait_ge(sem["setup_dve"], 33)
                else:
                    act.wait_ge(sem["xr_done"], j)
                for n in range(G_CONV):
                    act.wait_ge(sem["g_ready"], u + n + 1)
                    act.activation(y[:, n // 2, (n % 2) * HALF:(n % 2 + 1) * HALF], g[n % 2][:, :],
                                   ACT.Identity).then_inc(sem["y_copied"], 1)

            def silu(j):
                act.wait_ge(sem["coefs_done"], j + 1)
                for k in range(3):
                    act.activation(y[:, k, :], y[:, k, :], ACT.Silu, bias=coef[:, 1, k:k + 1],
                                   scale=coef[:, 0, k:k + 1]).then_inc(sem["silu_done"], 1)

            def window(j):
                act.wait_ge(sem["coef_shift"], 2 * j + 2)
                if not (isinstance(j, int) and j == 0):
                    act.wait_ge(sem["g_ready"], qkv_use(j - 1) + G_QKV)
                else:
                    act.wait_ge(sem["setup_dve"], 33)
                src = xr[:, :].rearrange("p (wy r wx c) -> p wy r wx c", wy=ROWS, r=WS, wx=ROWS)
                dst = xw[:, :].rearrange("p (wy wx r c) -> p wy r wx c", wy=ROWS, r=WS, wx=ROWS)
                for wy in range(ROWS):
                    last = act.activation(dst[:, wy], src[:, wy], ACT.Identity, bias=coef2[:, 1:2],
                                          scale=coef2[:, 0:1])
                last.then_inc(sem["xw_done"], 1)

            def step(b, has1, has2):
                u = qkv_use(b)
                for n, (dst, col, s, used, each) in enumerate(((qhl, BQ, "q_hi", "q_saved", 16), (khl, BK, "k_hi", "k_split", 1))):
                    act.wait_ge(sem[used], each * b)
                    for h in range(2):
                        act.wait_ge(sem["g_ready"], u + 2 * n + h + 1)
                        act.activation(dst[:, 0, h * HALF:(h + 1) * HALF], g[h][:, :], ACT.Identity,
                                       bias=w[:, col:col + 1]).then_inc(sem[s], 1)
                act.wait_ge(sem["v_turned"], b)
                for h in range(2):
                    act.wait_ge(sem["g_ready"], u + 4 + h + 1)
                    act.activation(vn[:, h * HALF:(h + 1) * HALF], g[h][:, :], ACT.Identity,
                                   bias=w[:, BV:BV + 1]).then_inc(sem["v_done"], 1)
                act.wait_ge(sem["pv_done"], PAIRS * b)
                for h in range(2):
                    act.wait_ge(sem["g_ready"], u + 6 + h + 1)
                    for par in range(2):
                        rows = slice(TOK * par, TOK * par + TOK)
                        act.activation(vp[rows, PAIRS * h:PAIRS * (h + 1), :, HD * par:HD * par + HD],
                                       g[h][rows, :].rearrange("p (w i c) -> p w i c", w=PAIRS, i=Q),
                                       ACT.Identity).then_inc(sem["vp_done"], 1)
                if has1:
                    copy_y(b + 1)
                for p in range(PAIRS):
                    s = PAIRS * b + p
                    if has1 and p == 2:
                        silu(b + 1)
                    if has2 and p == 6:
                        normalise(b + 2)
                    act.wait_ge(sem["st_ready"], s + 1)
                    act.wait_ge(sem["pv_done"], PAIRS * b + max(p - 1, 0))
                    act.activation(pt[:, p % 2].rearrange("p w i n -> p (w i n)"), tbk[p % 2][:, :],
                                   ACT.Exp).then_inc(sem["exp_done"], 1)
                if has1:
                    window(b + 1)

            normalise(0)
            copy_y(0)
            silu(0)
            normalise(1)
            window(0)
            images(act, step)

            for c in range(QD):
                act.wait_ge(sem["dw_ready"], c + 1)
                src = (sbk + tbk)[c % 4]
                act.activation(vt[:, c * SLOT:c * SLOT + 512], src[:, :], ACT.Identity).then_inc(sem["dw_copied"], 1)

        @block.vector
        def _(dve):
            v = nc.vector
            step_no = [0]

            def link(ins):
                step_no[0] += 1
                ins.then_inc(sem["setup_dve"], 1)
                dve.wait_ge(sem["setup_dve"], step_no[0])

            dve.wait_ge(sem["w_loaded"], 64)
            link(v.tensor_copy(sel[:, :], tc[0:2 * HEADS, SEL:SEL + Q * C]))
            link(v.tensor_copy(ident2[:, :], tc[:, ID2:ID2 + C]))
            for b in range(B):
                dve.wait_ge(x_loaded[b // 4], 16)
                v.bn_stats(sst[:, 2 * b, :], xall[:, b, 0:HALF])
                last = v.bn_stats(sst[:, 2 * b + 1, :], xall[:, b, HALF:PIX])
            link(last)
            for b in range(B):
                last = v.bn_aggr(smv[:, b, :], sst[:, 2 * b:2 * b + 2, :].rearrange("p a s -> p (a s)"))
            link(last)
            link(v.tensor_tensor(ssq[:, :], smv[:, :, 0], smv[:, :, 0], ALU.mult))
            link(v.tensor_tensor(sgs[:, :, 1], smv[:, :, 1], ssq[:, :], ALU.add))
            v.tensor_scalar(ssq[:, :], smv[:, :, 1], PIX / (PIX - 1.0), None, ALU.mult)
            link(v.tensor_copy(sgs[:, :, 0], smv[:, :, 0]))
            dve.wait_ge(sem["sm_ready"], 1)
            v.tensor_copy(sgs[:, :, :].rearrange("p b t -> p (b t)"), sm[:, 0:2 * B]).then_inc(sem["setup_read"], 1)
            dve.wait_ge(sem["setup_read"], 1)
            v.tensor_tensor(sva[:, :], sgs[:, :, 0], sgs[:, :, 0], ALU.mult).then_inc(sem["group_square"], 1)
            dve.wait_ge(sem["group_square"], 1)
            link(v.scalar_tensor_tensor(out=sva[:, :], in0=sgs[:, :, 1], scalar=EPS, in1=sva[:, :],
                                        op0=ALU.add, op1=ALU.subtract))
            dve.wait_ge(sem["setup_pool"], 2)
            v.tensor_copy(gn0[:, 0, :], srs[:, 0:B])
            link(v.scalar_tensor_tensor(out=gn0[:, 1, :], in0=sgs[:, :, 0], scalar=-1.0, in1=srs[:, 0:B],
                                        op0=ALU.mult, op1=ALU.mult))
            link(v.tensor_tensor(sva[:, :], smv[:, :, 0], sgs[:, :, 0], ALU.subtract))
            v.tensor_tensor(smv[:, :, 0], sva[:, :], srs[:, 0:B], ALU.mult)
            link(v.tensor_tensor(smv[:, :, 1], srs[:, B:2 * B], srs[:, 0:B], ALU.mult))
            dve.wait_ge(sem["sm_ready"], 2)
            v.tensor_copy(rs[:, 0:8], sm[0:B, 0:E]).then_inc(sem["setup_read"], 1)
            dve.wait_ge(sem["setup_read"], 2)
            link(v.tensor_copy(rs[:, 40:48], rs[:, 0:8]))
            for n in range(2):
                if n:
                    link(v.tensor_scalar(rs[:, 0:8], rs[:, 24:32], 30.0, -30.0, ALU.min, ALU.max))
                link(v.tensor_reduce(rs[:, 18:19], rs[:, 0:8], AX.X, ALU.max))
                link(v.tensor_scalar(rs[:, 16:17], rs[:, 18:19], -1.0, None, ALU.mult))
                dve.wait_ge(sem["setup_act"], 3 + n)
                link(v.reciprocal(rs[:, 19:20], rs[:, 17:18]))
                link(v.tensor_scalar(rs[:, 24:32], rs[:, 8:16], rs[:, 19:20], None, ALU.mult))
            link(v.max(rs[:, 32:40], rs[:, 24:32]))
            link(v.max_index(ri[:, :], rs[:, 32:40], rs[:, 24:32]))
            link(v.tensor_tensor(rs[:, 20:21], rs[:, 32:33], rs[:, 33:34], ALU.add))
            link(v.tensor_scalar(rs[:, 21:22], rs[:, 20:21], 1e-6, None, ALU.add))
            link(v.reciprocal(rs[:, 22:23], rs[:, 21:22]))
            v.tensor_scalar(rs[:, 48:50], rs[:, 32:34], rs[:, 22:23], None, ALU.mult)
            link(v.tensor_copy(rs[:, 50:52], ri[:, 0:2]))
            for b in range(B):
                last = v.tensor_scalar(rb[:, b, :], rs[:, 48:52], tc[0:B, EYE + b:EYE + b + 1], None, ALU.mult)
            link(last)
            dve.wait_ge(sem["sm_ready"], 3)
            v.tensor_copy(route[:, :, :].rearrange("p b t -> p (b t)"), sm[:, 0:4 * B]).then_inc(sem["setup_read"], 1)
            dve.wait_ge(sem["setup_read"], 3)
            link(v.tensor_copy(identb[:, :], tc[:, ID:ID + C]))
            link(v.tensor_scalar(w[:, WQ:WQ + C], w[:, WQ:WQ + C], HD ** -0.5, None, ALU.mult))
            link(v.tensor_copy(rnum[:, :], route[0:1, :, :].rearrange("p b t -> p (b t)")))
            dve.wait_ge(sem["setup_act"], 2)
            src = xw[:, 0:512].rearrange("p (m h) -> p h m", h=HEADS)
            dst = bias[:, :].rearrange("p (h m) -> p h m", h=HEADS)
            link(v.tensor_scalar(dst, src, 16.0, None, ALU.mult))
            link(v.scalar_tensor_tensor(out=dst[TOK:C], in0=src[TOK:C], scalar=16.0, in1=dst[TOK:C],
                                        op0=ALU.mult, op1=ALU.subtract))
            dve.wait_ge(sem["sm_ready"], 4)
            v.tensor_tensor(btot[:, :], sm[:, 0:1], w[:, BP:BP + 1], ALU.add).then_inc(sem["setup_read"], 1)
            dve.wait_ge(sem["setup_read"], 4)
            link(v.tensor_scalar(w[:, BQ:BQ + 1], w[:, BQ:BQ + 1], HD ** -0.5, None, ALU.mult))

            def group_sums(j, n, count):
                v.tensor_tensor(sq[:, 0:count], mv[:, 0:count, 0], mv[:, 0:count, 0],
                                ALU.mult).then_inc(sem["squares_done"], 1)
                dve.wait_ge(sem["squares_done"], 2 * j + n + 1)
                v.tensor_tensor(mv[:, 0:count, 1], mv[:, 0:count, 1], sq[:, 0:count],
                                ALU.add).then_inc(sem["sums_done"], 1)

            def group_variance(j, n, count, use):
                dve.wait_ge(sem["sm_ready"], use)
                v.tensor_copy(gs[:, 0:count, :].rearrange("p k t -> p (k t)"),
                              sm[:, 0:2 * count]).then_inc(sem["group_read"], 1)
                dve.wait_ge(sem["group_read"], 2 * j + n + 1)
                v.tensor_tensor(sq[:, 0:count], gs[:, 0:count, 0], gs[:, 0:count, 0],
                                ALU.mult).then_inc(sem["group_square"], 1)
                dve.wait_ge(sem["group_square"], 2 * j + n + 2)
                v.scalar_tensor_tensor(out=var[:, 0:count], in0=gs[:, 0:count, 1], scalar=EPS,
                                       in1=sq[:, 0:count], op0=ALU.add,
                                       op1=ALU.subtract).then_inc(sem["group_var"], 1)

            def y_stats(j):
                for n in range(G_CONV):
                    dve.wait_ge(sem["y_copied"], 6 * j + n + 1)
                    last = v.bn_stats(st[:, n, :], y[:, n // 2, (n % 2) * HALF:(n % 2 + 1) * HALF])
                last.then_inc(sem["bn_done"], 1)
                dve.wait_ge(sem["bn_done"], 2 * j + 1)
                dve.sem_inc(sem["settled_dve"], 1)
                for k in range(3):
                    last = v.bn_aggr(mv[:, k, :], st[:, 2 * k:2 * k + 2, :].rearrange("p a s -> p (a s)"))
                last.then_inc(sem["aggr_done"], 1)
                dve.wait_ge(sem["aggr_done"], 2 * j + 1)
                group_sums(j, 0, 3)

            def y_coefs(j):
                dve.wait_ge(sem["rstd_done"], 2 * j + 1)
                dve.wait_ge(sem["chosen"], j + 1)
                if not (isinstance(j, int) and j == 0):
                    dve.wait_ge(sem["silu_done"], 3 * j)
                v.tensor_tensor(coef[:, 0, :], rstd[:, :], gb[:, 0, :], ALU.mult).then_inc(sem["coef_scale"], 1)
                dve.wait_ge(sem["coef_scale"], 2 * j + 1)
                v.tensor_tensor(shift[:, :], gs[:, :, 0], coef[:, 0, :], ALU.mult).then_inc(sem["coef_shift"], 1)
                dve.wait_ge(sem["coef_shift"], 2 * j + 1)
                v.tensor_tensor(coef[:, 1, :], gb[:, 1, :], shift[:, :], ALU.subtract).then_inc(sem["coefs_done"], 1)

            def residual(j):
                wk = [(route[:, j, k:k + 1] if isinstance(j, int)
                       else route[:, :, :].rearrange("p b t -> p (b t)")[:, bass.ds(4 * j + k, 1)]) for k in range(TOP)]
                dve.wait_ge(sem["silu_done"], 3 * j + 3)
                if not (isinstance(j, int) and j == 0):
                    dve.wait_ge(sem["x1_copied"], j)
                    dve.wait_ge(sem["xw_done"], j)
                v.tensor_tensor(xr[:, :], y[:, 0, :], xin[:, :], ALU.add).then_inc(sem["sum_shared"], 1)
                dve.wait_ge(sem["sum_shared"], j + 1)
                v.scalar_tensor_tensor(out=xr[:, :], in0=y[:, 1, :], scalar=wk[0], in1=xr[:, :],
                                       op0=ALU.mult, op1=ALU.add).then_inc(sem["sum_first"], 1)
                dve.wait_ge(sem["sum_first"], j + 1)
                v.scalar_tensor_tensor(out=xr[:, :], in0=y[:, 2, :], scalar=wk[1], in1=xr[:, :],
                                       op0=ALU.mult, op1=ALU.add).then_inc(sem["xr_done"], 1)
                dve.wait_ge(sem["xr_done"], j + 1)
                for h in range(2):
                    last = v.bn_stats(st[:, h, :], xr[:, h * HALF:(h + 1) * HALF])
                last.then_inc(sem["bn_done"], 1)
                dve.wait_ge(sem["bn_done"], 2 * j + 2)
                dve.sem_inc(sem["settled_dve"], 1)
                v.bn_aggr(mv[:, 0, :], st[:, 0:2, :].rearrange("p a s -> p (a s)")).then_inc(sem["aggr_done"], 1)
                dve.wait_ge(sem["aggr_done"], 2 * j + 2)
                group_sums(j, 1, 1)

            def x_coefs(j):
                dve.wait_ge(sem["rstd_done"], 2 * j + 2)
                v.tensor_copy(coef2[:, 0:1], rstd[:, 0:1]).then_inc(sem["coef_scale"], 1)
                v.scalar_tensor_tensor(out=coef2[:, 1:2], in0=gs[:, 0, 0:1], scalar=-1.0, in1=rstd[:, 0:1],
                                       op0=ALU.mult, op1=ALU.mult).then_inc(sem["coef_shift"], 1)

            def maxima(b, p):
                s = PAIRS * b + p
                dve.wait_ge(sem["s_ready"], s + 1)
                v.tensor_reduce(mx[:, :], sbk[p % 2][:, :].rearrange("p (h m) -> p h m", h=HEADS), AX.X,
                                ALU.max).then_inc(sem["s_max"], 1)
                dve.wait_ge(sem["s_max"], s + 1)
                v.tensor_copy(cm[:, 0:HEADS], mx[:, :]).then_inc(sem["c_hi"], 1)
                dve.wait_ge(sem["c_hi"], s + 1)
                v.tensor_tensor(cm[:, HEADS:2 * HEADS], mx[:, :], cm[:, 0:HEADS], ALU.subtract).then_inc(sem["c_lo"], 1)

            def outputs(b, r):
                n = ROWS * b + r
                dve.wait_ge(sem["pv_done"], PAIRS * b + 2 * r + 2)
                v.reciprocal(rec[:, :], pvb[:, WROW:2 * WROW]).then_inc(sem["recip_done"], 1)
                dve.wait_ge(sem["recip_done"], n + 1)
                if r == 0 and not (isinstance(b, int) and b == 0):
                    dve.wait_ge(sem["acc_done"], 2 * b)
                v.tensor_tensor(o[:, r * WROW:(r + 1) * WROW].rearrange("p (r x c) -> p x r c", r=WS, x=ROWS),
                                pvb[:, 0:WROW].rearrange("p (x r c) -> p x r c", r=WS, x=ROWS),
                                rec[:, :].rearrange("p (x r c) -> p x r c", r=WS, x=ROWS),
                                ALU.mult).then_inc(sem["o_done"], 1)

            def step(b, has1, has2):
                for dst, col, hi, lo in ((qhl, BQ, "q_hi", "q_lo"), (khl, BK, "k_hi", "k_lo")):
                    for h in range(2):
                        dve.wait_ge(sem[hi], 2 * b + h + 1)
                        part = slice(h * HALF, (h + 1) * HALF)
                        v.scalar_tensor_tensor(out=dst[:, 1, part], in0=g[h][:, :], scalar=w[:, col:col + 1],
                                               in1=dst[:, 0, part], op0=ALU.add, op1=ALU.subtract
                                               ).then_inc(sem[lo], 1)
                dve.wait_ge(sem["k_lo"], 2 * b + 2)
                dve.wait_ge(sem["k_saved"], 16 * b)
                for t in range(2):
                    for par in range(2):
                        last = v.tensor_scalar(kpar[:, t, :, par, :], khl[:, t, :].rearrange("p (w m) -> p w m", m=TOK),
                                               cc[:, PM + par:PM + par + 1], None, ALU.mult)
                last.then_inc(sem["k_split"], 1)
                dve.wait_ge(sem["v_done"], 2 * b + 2)
                dve.wait_ge(sem["vt_done"], b)
                v.transpose(vtmp[:, :].rearrange("p (c y) -> p y c", c=QD),
                            vn[:, :].rearrange("p (y x) -> p y x", x=W)[:, :, ::-1]).then_inc(sem["v_turned"], 1)
                slots = small_slots(b)
                if has1:
                    y_stats(b + 1)
                maxima(b, 0)
                for p in range(PAIRS):
                    s = PAIRS * b + p
                    dve.wait_ge(sem["sm_ready"], sm_use(b, slots[f"max{p}"]))
                    dve.wait_ge(sem["st_ready"], s)
                    v.tensor_copy(ct[:, :], smb[0:2 * HEADS, 0:C]).then_inc(sem["ct_done"], 1)
                    if p < PAIRS - 1:
                        maxima(b, p + 1)
                    if p % 2 == 0 and p:
                        outputs(b, p // 2 - 1)
                    if has1 and p == 0:
                        group_variance(b + 1, 0, 3, sm_use(b, slots["gn_y"]))
                        y_coefs(b + 1)
                    if has1 and p == 3:
                        residual(b + 1)
                    if has1 and p == 5:
                        group_variance(b + 1, 1, 1, sm_use(b, slots["gn_x"]))
                        x_coefs(b + 1)
                outputs(b, ROWS - 1)
                u = proj_use(b)
                for h in range(2):
                    dve.wait_ge(sem["g_ready"], u + h + 1)
                    dve.wait_ge(sem["x1_copied"], b + 1)
                    part = slice(h * HALF, (h + 1) * HALF)
                    v.scalar_tensor_tensor(out=x1[:, part], in0=g[h][:, :], scalar=btot[:, 0:1], in1=x1[:, part],
                                           op0=ALU.add, op1=ALU.add).then_inc(sem["acc_done"], 1)

            y_stats(0)
            group_variance(0, 0, 3, SM_SETUP + 1)
            y_coefs(0)
            residual(0)
            group_variance(0, 1, 1, SM_SETUP + 2)
            x_coefs(0)
            images(dve, step)

            def turn_back(b):
                dve.wait_ge(sem["dw_copied"], QD)
                if b >= 2:
                    dve.wait_ge(sem["g_ready"], LAST_USE + 2 * (b - 1))
                src = vt[:, :].rearrange("p (c s) -> p s c", c=QD)[:, H * b:H * b + H, :]
                v.transpose((vn, vtmp)[b % 2][:, :].rearrange("p (y x) -> p y x", x=W), src
                            ).then_inc(sem["pe_turned"], 1)

            turn_back(0)
            for b in range(B):
                if b + 1 < B:
                    turn_back(b + 1)
                dve.wait_ge(sem["acc_loaded"], 16 * min(b + 2, B) if b + 2 <= B else 16 * B)
                if b >= 2:
                    dve.wait_ge(sem["stored"], 16 * (b - 1))
                for h in range(2):
                    dve.wait_ge(sem["g_ready"], LAST_USE + 2 * b + h + 1)
                    part = slice(h * HALF, (h + 1) * HALF)
                    v.tensor_tensor((xr, x1)[b % 2][:, part], g[h][:, :], (xin, xw)[b % 2][:, part],
                                    ALU.add).then_inc(sem["out_done"], 1)

        @block.tensor
        def _(pe):
            mm = nc.tensor.matmul
            pe.wait_ge(sem["w_loaded"], 64)
            for n, bk in enumerate((tbk[0], sbk[0])):
                at = TBL + n * TABLE // 2
                last = mm(bk[:, 0:TABLE // 2], l1s[:, :], tc[0:3, at:at + TABLE // 2], start=True, stop=True)
            last.then_inc(sem["setup_pe"], 1)
            pe.wait_ge(sem["setup_act"], 1)
            for m in range(TOK):
                at = (WS - 1 - m % WS) * REL * WS + (WS - 1 - m // WS) * WS
                for part in range(2):
                    last = mm(tbk[1][TOK * part:TOK * part + TOK, HEADS * m:HEADS * m + HEADS],
                              hb[:, at:at + TOK], w[:, CW2:CW2 + HEADS], start=True, stop=True)
            last.then_inc(sem["setup_pe"], 1)
            pe.wait_ge(sem["setup_dve"], 7)
            mm(sm[:, 0:2 * B], cc[:, AV4:AV4 + C], sgs[:, :, :].rearrange("p b t -> p (b t)"), start=True,
               stop=True).then_inc(sem["sm_ready"], 1)
            pe.wait_ge(sem["setup_dve"], 11)
            mm(sm[0:B, 0:E], smv[:, :, 0], w[:, RWM:RWM + E], start=True, stop=False)
            mm(sm[0:B, 0:E], smv[:, :, 1], w[:, RWS:RWS + E], start=False, stop=True).then_inc(sem["sm_ready"], 1)
            pe.wait_ge(sem["setup_dve"], 28)
            mm(sm[:, 0:4 * B], tc[0:B, ONE:ONE + C], rb[:, :, :].rearrange("p b t -> p (b t)"), start=True,
               stop=True).then_inc(sem["sm_ready"], 1)
            pe.wait_ge(sem["setup_read"], 3)
            mm(sm[:, 0:1], w[:, WP:WP + C], w[:, BV:BV + 1], start=True, stop=True).then_inc(sem["sm_ready"], 1)
            pe.wait_ge(sem["setup_dve"], 34)

            def convolve(j):
                first = isinstance(j, int) and j == 0
                pe.wait_ge(sem["xn_done"], j + 1)
                for h in range(2):
                    if not first:
                        pe.wait_ge(sem["vp_done"], 4 * (j - 1) + 2 * h + 2)
                    mm(g[h][:, :], w[:, WSH:WSH + C], xn[:, 1 + 16 * h:17 + 16 * h, 1:W + 1], start=True,
                       stop=True).then_inc(sem["g_ready"], 1)
                pe.wait_ge(sem["rows_loaded"], 32 * TOP * (j + 1))
                pe.wait_ge(sem["chosen_w"], 16 * TOP * (j + 1))
                for k in range(TOP):
                    for h in range(2):
                        pe.wait_ge(sem["y_copied"], 6 * j + 2 * k + h + 1)
                        for dy in range(2):
                            last = mm(g[h][:, :], wsel[:, k, C * dy:C * dy + C],
                                      xsh[:, k, dy + 16 * h:dy + 16 * h + 16, 0:W], start=(dy == 0), stop=(dy == 1))
                        last.then_inc(sem["g_ready"], 1)

            def average(j, n, count, before, col):
                pe.wait_ge(sem["sums_done"], 2 * j + n + 1)
                if not (isinstance(j, int) and j == 0):
                    pe.wait_ge(sem["ct_done"], before)
                elif n:
                    pe.wait_ge(sem["group_read"], 1)
                mm(sm[:, 0:2 * count], cc[:, col:col + C], mv[:, 0:count, :].rearrange("p k t -> p (k t)"),
                   start=True, stop=True).then_inc(sem["sm_ready"], 1)

            def project_in(b):
                pe.wait_ge(sem["xw_done"], b + 1)
                pe.wait_ge(sem["acc_done"], 2 * b)
                pe.wait_ge(sem["y_copied"], G_CONV * b + G_CONV)
                for n, col in enumerate((WQ, WK)):
                    for h in range(2):
                        if n:
                            pe.wait_ge(sem["q_lo"], 2 * b + h + 1)
                        mm(g[h][:, :], w[:, col:col + C], xw[:, h * HALF:(h + 1) * HALF], start=True,
                           stop=True).then_inc(sem["g_ready"], 1)
                nat = xw[:, :].rearrange("p (wy wx r c) -> p wy r wx c", wy=ROWS, r=WS, wx=ROWS)
                for h in range(2):
                    pe.wait_ge(sem["k_lo"], 2 * b + h + 1)
                    for k in range(2):
                        last = mm(g[h][:, k * WROW:(k + 1) * WROW], w[:, WV:WV + C], nat[:, 2 * h + k],
                                  start=True, stop=True)
                    last.then_inc(sem["g_ready"], 1)
                wv = w[:, WV:WV + C].rearrange("p (i t c) -> p t i c", i=Q, t=2)
                for h in range(2):
                    pe.wait_ge(sem["v_done"], 2 * b + h + 1)
                    for n in range(PAIRS):
                        win = PAIRS * h + n
                        for par in range(2):
                            last = mm(g[h][TOK * par:TOK * par + TOK, n * TOK:n * TOK + TOK],
                                      xw[:, win * TOK:win * TOK + TOK], wv[:, par], start=True, stop=True)
                    last.then_inc(sem["g_ready"], 1)

            def scores(b, p):
                s = PAIRS * b + p
                if p == 0:
                    pe.wait_ge(sem["q_stacked"], 48 * b + 48)
                    pe.wait_ge(sem["k_stacked"], 48 * b + 48)
                pe.wait_ge(sem["s_max"], PAIRS * b + max(p - 1, 0))
                bk = sbk[p % 2]
                mm(bk[:, :], ident2[:, :], bias[:, :], start=True, stop=False, skip_group_check=True)
                for i in range(Q):
                    for n in range(2):
                        at = (2 * p + n) * TOK
                        last = mm(bk[TOK * n:TOK * n + TOK, C * i:C * i + C], qs[0:3 * QD, i, at:at + TOK],
                                  ks[0:3 * QD, i, 2 * at:2 * at + C], start=False, stop=(i == Q - 1), skip_group_check=True)
                last.then_inc(sem["s_ready"], 1)

            def turned_scores(b, p):
                s = PAIRS * b + p
                pe.wait_ge(sem["exp_done"], PAIRS * b + max(p - 1, 0))
                bk = tbk[p % 2][:, :].rearrange("p (w i n) -> p i w n", w=2, i=Q)
                for i in range(Q):
                    mm(bk[:, i], bias[:, C * i:C * i + C], ident2[:, :], start=(i == 0), stop=False,
                       skip_group_check=True)
                for i in range(Q):
                    for n in range(2):
                        at = (2 * p + n) * TOK
                        mm(bk[:, i, n], ks[0:3 * QD, i, 2 * at:2 * at + C], qs[0:3 * QD, i, at:at + TOK],
                           start=False, stop=False, skip_group_check=True)
                pe.wait_ge(sem["ct_done"], s + 1)
                for i in range(Q):
                    last = mm(bk[:, i], sel[:, C * i:C * i + C], ct[:, :], start=False, stop=(i == Q - 1),
                              skip_group_check=True)
                last.then_inc(sem["st_ready"], 1)

            def values(b, p):
                s = PAIRS * b + p
                pe.wait_ge(sem["exp_done"], s + 1)
                if p == 0:
                    pe.wait_ge(sem["vp_done"], 4 * b + 4)
                if p % 2 == 0:
                    pe.wait_ge(sem["o_done"], ROWS * b + p // 2)
                at = (p % 2) * 2 * TOK
                for n in range(2):
                    for i in range(Q):
                        mm(pvb[QD * i:QD * i + QD, at + n * TOK:at + n * TOK + TOK], vp[:, 2 * p + n, i, :],
                           pt[:, p % 2, n, i, :], start=True, stop=True)
                for i in range(Q):
                    last = mm(pvb[QD * i:QD * i + QD, WROW + at:WROW + at + 2 * TOK], cc[:, OM:OM + QD],
                              pt[:, p % 2, :, i, :], start=True, stop=True)
                last.then_inc(sem["pv_done"], 1)

            def turn_maxima(b, p, has1):
                pe.wait_ge(sem["c_lo"], PAIRS * b + p + 1)
                pe.wait_ge(sem["ct_done"], PAIRS * b + p)
                pe.wait_ge(sem["group_read"], 2 * b + 2 + (((p > 0) + (p > 5)) if has1 else 0))
                nc.tensor.transpose(smb[0:2 * HEADS, 0:C], cm[:, :], identb[:, :]).then_inc(sem["sm_ready"], 1)

            def step(b, has1, has2):
                project_in(b)
                if has1:
                    convolve(b + 1)
                scores(b, 0)
                for p in range(PAIRS):
                    if p + 1 < PAIRS:
                        scores(b, p + 1)
                    if has1 and p == 6:
                        average(b + 1, 1, 1, PAIRS * b + 6, AV4)
                    turn_maxima(b, p, has1)
                    if p:
                        values(b, p - 1)
                    if has1 and p == 0:
                        average(b + 1, 0, 3, PAIRS * b + 1, AV16)
                    turned_scores(b, p)
                values(b, PAIRS - 1)
                pe.wait_ge(sem["o_done"], ROWS * b + ROWS)
                for h in range(2):
                    if has1:
                        pe.wait_ge(sem["y_copied"], G_CONV * (b + 1) + 2 * TOP + h + 1)
                    else:
                        pe.wait_ge(sem["vp_done"], 4 * b + 2 * h + 2)
                    mm(g[h][:, :], w[:, WP:WP + C], o[:, h * HALF:(h + 1) * HALF], start=True,
                       stop=True).then_inc(sem["g_ready"], 1)

            convolve(0)
            average(0, 0, 3, 0, AV16)
            average(0, 1, 1, 0, AV4)
            images(pe, step)

            for c in range(QD):
                pe.wait_ge(tap_loaded[c % 4], 16 * Q * (c // 4 + 1))
                if c >= 4:
                    pe.wait_ge(sem["dw_copied"], c - 3)
                else:
                    pe.wait_ge(sem["vt_done"], B)
                bk = (sbk + tbk)[c % 4]
                for dy in range(DWK):
                    last = mm(bk[:, :], taps[:, c % 4, dy, :], vt4[:, c, :, dy:dy + H], start=(dy == 0),
                              stop=(dy == DWK - 1))
                last.then_inc(sem["dw_ready"], 1)
            for b in range(B):
                pe.wait_ge(sem["pe_turned"], b + 1)
                for h in range(2):
                    if b:
                        pe.wait_ge(sem["out_done"], 2 * (b - 1) + h + 1)
                    else:
                        pe.wait_ge(sem["acc_done"], 2 * (B - 1) + h + 1)
                    mm(g[h][:, :], w[:, WP:WP + C], (vn, vtmp)[b % 2][:, h * HALF:(h + 1) * HALF], start=True,
                       stop=True).then_inc(sem["g_ready"], 1)


def _lay_out(np, a):
    f = np.float32
    g = C // HEADS
    t = np.ascontiguousarray
    qkv = a["L1_conv_qkv_w"]
    shared = np.zeros((C, C), f)
    for n in range(HEADS):
        r = slice(g * n, g * n + g)
        shared[r, r] = a["L0_conv_shared_w"][r, :, 0, 0].T
    rw = a["L0_conv_router_w"]
    cols = [qkv[0:C].T, qkv[C:2 * C].T, qkv[2 * C:].T, a["L1_conv_proj_w"].T, shared, rw[:, 0:C].T, rw[:, C:].T,
            a["L1_conv_cpb_w2"].T, a["L0_conv_expert_g"].T, a["L0_conv_expert_b"].T]
    cols += [v.reshape(C, 1) for v in (a["L0_conv_gn_shared_g"], a["L0_conv_gn_shared_b"], a["L1_conv_qkv_b"][0:C],
                                      a["L1_conv_qkv_b"][C:2 * C], a["L1_conv_qkv_b"][2 * C:], a["L1_conv_proj_b"])]
    wa = t(np.concatenate(cols, axis=1))
    fused = a["L0_conv_fused_w"].reshape(E, C, GC, 3, 3).transpose(0, 3, 4, 2, 1)
    wx = np.zeros((E, 2, 3, GC, 2, C), f)
    wx[:, :, :, :, 0] = fused[:, 0:2]
    wx[:, 1, :, :, 1] = fused[:, 2]
    wx = wx.reshape(E, SH, 2 * C)
    dw = np.zeros((C, DWK, HANK), f)
    dw[:, :, W - 1 - PAD:W + PAD] = a["L1_conv_dw_w"][:, 0, :, ::-1]
    l1 = t(np.concatenate([a["L1_conv_cpb_w1"].T, a["L1_conv_cpb_b1"].reshape(1, C)], axis=0))
    n = np.arange(C)
    cst = np.zeros((C, CCOLS), f)
    cst[:, AV4:AV4 + C] = (n[:, None] // 4 == n[None] // 4) * 0.25
    cst[:, AV16:AV16 + C] = (n[:, None] // 16 == n[None] // 16) * 0.0625
    cst[:, OM:OM + QD] = n[:, None] // TOK == np.arange(QD)[None] // HD
    cst[:, PM:PM + 2] = n[:, None] // HD % 2 == np.arange(2)[None]
    tmp = np.zeros((C, TCOLS), f)
    tmp[:, ID:ID + C] = np.eye(C)
    tmp[:, ID2:ID2 + C] = n[:, None] % TOK == n[None] % TOK
    for r in range(2 * HEADS):
        i, par = (r % HEADS) // 2, r % 2
        tmp[r, SEL + C * i + TOK * par:SEL + C * i + TOK * par + TOK] = -1.0
    tmp[0:B, EYE:EYE + B] = np.eye(B)
    tmp[0:B, ONE:ONE + C] = 1.0
    r = np.arange(-(WS - 1), WS, dtype=f)
    grid = np.stack(np.meshgrid(r, r, indexing="ij"), axis=-1) / (WS - 1) * 8.0
    grid = (np.sign(grid) * np.log2(np.abs(grid) + 1.0) / np.log2(8.0)).astype(f).reshape(-1, 2)
    k = np.arange(TABLE)
    tmp[0:2, TBL:] = grid.T[:, (k // WS % REL) * REL + k // (WS * REL) + k % WS]
    tmp[2, TBL:] = 1.0
    return {"wa": wa, "wx": wx, "dw": dw, "l1": l1, "cst": cst, "tmp": tmp}


def kernel(**inputs):
    import numpy as np
    import concourse.bacc as bacc
    from concourse.bass_utils import run_bass_kernel_spmd as run

    arrays = {"x": np.ascontiguousarray(inputs["x"])}
    arrays.update(_lay_out(np, {k: np.asarray(v) for k, v in inputs.items()}))
    nc = bacc.Bacc("TRN2", target_bir_lowering=False, num_devices=1)
    args = {k: nc.dram_tensor(k, v.shape, mybir.dt.from_np(v.dtype), kind="ExternalInput").ap()
            for k, v in arrays.items()}
    out = nc.dram_tensor("out", (B, C, H, W), F32, kind="ExternalOutput").ap()
    program(nc, args["x"], args["wa"], args["wx"], args["dw"], args["l1"], args["cst"], args["tmp"], out)
    r = run(nc, [arrays], core_ids=[0])
    return r.results[0]["out"]
```

```python
from contextlib import ExitStack

import concourse.bass as bass
from concourse import mybir

F32 = mybir.dt.float32
F16 = mybir.dt.float16
BF16 = mybir.dt.bfloat16
I32 = mybir.dt.int32
U32 = mybir.dt.uint32
ALU = mybir.AluOpType
ACT = mybir.ActivationFunctionType
AX = mybir.AxisListType

B, C, H, W = 16, 128, 32, 32
PIX = H * W
HALF = PIX // 2
E = 8
TOP = 2
QD = 32
Q = C // QD
HEADS, HD = 8, 16
WS = 8
TOK = WS * WS
ROWS = H // WS
WROW = PIX // ROWS
PAIRS = (PIX // TOK) // 2
PAD = 3
HP = H + 2 * PAD
DWK = 7
HANK = 64
SLOT = B * HP
EPS = 1e-5
BN = float(1.0 / (1.0 + 1e-5) ** 0.5)
REL = 2 * WS - 1
GC = C // E
SH = 2 * 3 * GC
WPAD = W + 2
RUN = H * WPAD + W

WQ, WK, WV, WP, WSH = (C * n for n in range(5))
RWM = 5 * C
RWS = RWM + E
CW2 = RWS + E
EXG = CW2 + HEADS
EXB = EXG + E
VEC = EXB + E
SHG, SHB, BQ, BK, BV, BP = range(VEC, VEC + 6)
WCOLS = VEC + 6
AV4, AV16, OM = 0, C, 2 * C
PM = 2 * C + QD
CCOLS = PM + 2
ID, ID2, SEL, EYE, ONE, TBL = 0, C, 2 * C, 2 * C + 4 * C, 2 * C + 4 * C + B, 2 * C + 4 * C + B + C
TABLE = WS * REL * WS
TCOLS = TBL + TABLE

G_CONV, G_QKV, G_IMAGE = 6, 8, 16
SM_SETUP, SM_IMAGE = 4, PAIRS + 2
P_QK = 2
P_Y = 3
P_X = 5

SEMS = """
w_loaded x_loaded0 x_loaded1 x_loaded2 x_loaded3
setup_dve setup_act setup_pe setup_pool
xin_loaded xn_saved rows_loaded xn_done chosen chosen_w g_ready
y_copied bn_done aggr_done squares_done sums_done sm_ready setup_read group_read group_square group_var
rstd_done coef_scale coef_shift coefs_done silu_done sum_shared sum_first xr_done
xw_done xr_saved x1_loaded q_hi k_hi q_lo k_lo q_saved k_split k_split_hi k_saved stacked0 stacked1
v_done v_turned vt_done vp_done s_ready s_max mx_done c_hi c_lo ct_done st_ready exp_done pv_done
recip_done o_done acc_done acc_saved vt_clear
tap_zero tap_loaded0 tap_loaded1 tap_loaded2 tap_loaded3 dw_ready dw_copied pe_turned acc_loaded out_done stored settled_sp settled_pool settled_dve
""".split()


def program(nc, x, wa, wx, dw, l1, cst, tmp, out):
    with ExitStack() as ctx:
        def sb(name, shape, dt=F32):
            return ctx.enter_context(nc.sbuf_tensor(name, shape, dt))

        def bank(name):
            return ctx.enter_context(nc.psum_tensor(name, [C, 512], F32))

        vt = sb("vt", [C, QD * SLOT])
        vt4 = vt[:, :].rearrange("p (c b y) -> p c b y", c=QD, b=B)
        xall = vt[:, 0:B * PIX].rearrange("p (b n) -> p b n", b=B)
        xsh = sb("xsh", [SH, TOP, H + 1, WPAD])
        y = sb("y", [C, 3, PIX])
        tc = y[:, :, :].rearrange("p k n -> p (k n)")
        xin = sb("xin", [C, PIX])
        xn = sb("xn", [C, H + 2, WPAD])
        xr = sb("xr", [C, PIX])
        x1 = sb("x1", [C, PIX])
        xw = sb("xw", [C, PIX])
        vn = sb("vn", [C, PIX])
        vtmp = sb("vtmp", [C, PIX])
        o = sb("o", [C, PIX])
        qhl = sb("qhl", [C, 2, PIX], F16)
        khl = sb("khl", [C, 2, PIX], F16)
        kpar = sb("kpar", [C, 2, 2 * PAIRS, 2, TOK], F16)
        stack = sb("stack", [C, 3 * Q * PIX // 2])
        qs = stack[:, 0:Q * PIX // 2].bitcast(F16).rearrange("p (i n) -> p i n", i=Q)
        ks = stack[:, Q * PIX // 2:].bitcast(F16).rearrange("p (i n) -> p i n", i=Q)
        taps = stack[:, 0:4 * DWK * C].rearrange("p (s d m) -> p s d m", s=4, d=DWK)
        pt = sb("pt", [C, 2, 2, Q, TOK])
        vp = sb("vp", [C, 2 * PAIRS, Q, QD])
        wsel = sb("wsel", [SH, TOP, 2 * C])
        w = sb("w", [C, WCOLS])
        cc = sb("cc", [C, CCOLS])
        bias = sb("bias", [C, Q * C], F16)
        sel = sb("sel", [C, Q * C], BF16)
        ident2 = sb("ident2", [C, C], F16)
        identb = sb("identb", [C, C], BF16)
        rec = sb("rec", [C, WROW])
        gn0 = sb("gn0", [C, 2, B])
        route = sb("route", [C, B, 4])
        rnum = sb("rnum", [1, B * 4], I32)
        st = sb("st", [C, 6, 6])
        mv = sb("mv", [C, 3, 2])
        sq = sb("sq", [C, 3])
        gs = sb("gs", [C, 3, 2])
        var = sb("var", [C, 3])
        rstd = sb("rstd", [C, 3])
        power = sb("power", [C, 2, 2 * B])
        gb = sb("gb", [C, 2, 3])
        coef = sb("coef", [C, 2, 3])
        shift = sb("shift", [C, 3])
        coef2 = sb("coef2", [C, 2])
        mx = sb("mx", [C, HEADS])
        cm = sb("cm", [C, 2 * HEADS], BF16)
        ct = sb("ct", [C, C], BF16)
        btot = sb("btot", [C, 1])
        sst = sb("sst", [C, 2 * B, 6])
        smv = sb("smv", [C, B, 2])
        ssq = sb("ssq", [C, B])
        sva = sb("sva", [C, B])
        sgs = sb("sgs", [C, B, 2])
        srs = sb("srs", [C, 2 * B])
        rs = sb("rs", [B, 64])
        rb = sb("rb", [B, B, 4])
        ri = sb("ri", [B, 8], U32)
        l1s = sb("l1s", [3, C])
        hb = o[:, 0:TABLE]
        free = [y[:, n, :] for n in range(3)] + [xin[:, :], xr[:, :], x1[:, :], xw[:, :], o[:, :]]
        free += [t[:, :, :].rearrange("p t n -> p (t n)").bitcast(F32) for t in (qhl, khl)]
        free.append(pt[:, :, :, :, :].rearrange("p s w i n -> p (s w i n)"))
        free.append(xn[:, :, :].rearrange("p h w -> p (h w)")[:, 0:PIX])
        for t in (kpar[:, :, :, :, :].rearrange("p t w a m -> p (t w a m)").bitcast(F32),
                  vp[:, :, :, :].rearrange("p w i c -> p (w i c)")):
            free += [t[:, 0:PIX], t[:, PIX:2 * PIX]]
        acc = free[0:B]

        g = [bank("g0"), bank("g1")]
        sbk = [bank("s0"), bank("s1")]
        tbk = [bank("t0"), bank("t1")]
        pvb = bank("pv")
        sm = bank("sm")
        smb = sm[:, :].bitcast(BF16)

        xs = nc.dram_tensor("xs", [C, (H + 2) * WPAD], F32).ap()
        sq_d = nc.dram_tensor("sq_d", [2, C, PIX], F16).ap()
        sk_d = nc.dram_tensor("sk_d", [2, C, 2 * PIX], F16).ap()
        acc_d = nc.dram_tensor("acc_d", [B, C, PIX], F32).ap()

        sem = {n: ctx.enter_context(nc.semaphore(n)) for n in SEMS}
        tap_loaded = [sem[f"tap_loaded{n}"] for n in range(4)]
        stacked = [sem["stacked0"], sem["stacked1"]]
        x_loaded = [sem[f"x_loaded{n}"] for n in range(4)]

        def use_base(b):
            last = isinstance(b, int) and b == B - 1
            return 2 * G_CONV + G_QKV + G_IMAGE * b - (G_CONV if last else 0)

        def conv_use(j):
            if isinstance(j, int) and j < 2:
                return (G_CONV + G_QKV) * j
            return use_base(j - 2)

        def qkv_use(j):
            if isinstance(j, int) and j == 0:
                return G_CONV
            last = isinstance(j, int) and j == B - 1
            return use_base(j - 1) + (0 if last else G_CONV)

        def proj_use(b):
            if isinstance(b, int) and b >= B - 2:
                return use_base(b) + (G_QKV if b == B - 2 else 0)
            return use_base(b) + G_CONV + G_QKV

        LAST_USE = proj_use(B - 1) + 2

        def small_slots(b):
            names = [f"max{p}" for p in range(PAIRS)]
            if not (isinstance(b, int) and b >= B - 2):
                names.insert(P_Y + 1, "gn_y")
                names.append("gn_x")
            return {n: k for k, n in enumerate(names)}

        def sm_use(b, name):
            before = SM_IMAGE * b - (2 if isinstance(b, int) and b == B - 1 else 0)
            return SM_SETUP + 5 + small_slots(b)[name] + before

        def images(eng, step):
            step(0, True, True, True)
            with eng.Fori(1, B - 3) as b:
                step(b, True, True, True)
            step(B - 3, True, True, False)
            step(B - 2, True, False, False)
            step(B - 1, False, False, False)

        block = ctx.enter_context(nc.Block())

        @block.sync
        def _(sp):
            xb = x.rearrange("b c h w -> c b (h w)")
            sp.dma_start(w[:, :], wa).then_inc(sem["w_loaded"], 16)
            sp.dma_start(cc[:, :], cst).then_inc(sem["w_loaded"], 16)
            sp.dma_start(tc[:, 0:TCOLS], tmp).then_inc(sem["w_loaded"], 16)
            sp.dma_start(l1s[:, :], l1).then_inc(sem["w_loaded"], 16)
            for n in range(4):
                sp.dma_start(xall[:, 4 * n:4 * n + 4, :], xb[:, 4 * n:4 * n + 4, :]).then_inc(x_loaded[n], 16)

            def save_qk(j):
                sp.wait_ge(sem["q_lo"], 2 * j + 2)
                sp.sem_inc(sem["settled_sp"], 1)
                if not (isinstance(j, int) and j == 0):
                    sp.wait_ge(sem["stacked1"], 96 * j)
                    sp.sem_inc(sem["settled_sp"], 1)
                sp.dma_start(sq_d.rearrange("t c n -> c t n"), qhl[:, :, :]).then_inc(sem["q_saved"], 16)
                sp.wait_ge(sem["k_split_hi"], j + 1)
                sp.sem_inc(sem["settled_sp"], 1)
                sp.wait_ge(sem["k_split"], j + 1)
                sp.sem_inc(sem["settled_sp"], 1)
                sp.dma_start(sk_d.rearrange("t c n -> c t n"),
                             kpar[:, :, :, :, :].rearrange("p t w a m -> p t (w a m)")).then_inc(sem["k_saved"], 16)

            def stack_qk(j, half):
                if half == 0:
                    sp.wait_ge(sem["q_saved"], 16 * j + 16)
                    sp.sem_inc(sem["settled_sp"], 1)
                    sp.wait_ge(sem["k_saved"], 16 * j + 16)
                    sp.sem_inc(sem["settled_sp"], 1)
                if not (isinstance(j, int) and j == 0):
                    sp.wait_ge(sem["st_ready"], PAIRS * (j - 1) + PAIRS // 2 * (half + 1))
                    sp.sem_inc(sem["settled_sp"], 1)
                n, m = HALF * half, 2 * HALF * half
                for part, t in enumerate((0, 1, 0)):
                    sp.dma_start(qs[QD * part:QD * part + QD, :, n:n + HALF],
                                 sq_d[t, :, n:n + HALF].rearrange("(i c) n -> c i n", i=Q)).then_inc(stacked[half], 16)
                for part, t in enumerate((0, 0, 1)):
                    sp.dma_start(ks[QD * part:QD * part + QD, :, m:m + 2 * HALF],
                                 sk_d[t, :, m:m + 2 * HALF].rearrange("(i c) n -> c i n", i=Q)).then_inc(stacked[half], 16)

            def image_acc(b):
                return acc_d[b] if isinstance(b, int) else acc_d[bass.ds(b, 1)].rearrange("b c n -> c (b n)")

            def save_xr(j):
                sp.wait_ge(sem["xr_done"], j + 1)
                sp.sem_inc(sem["settled_sp"], 1)
                sp.dma_start(image_acc(j), xr[:, :]).then_inc(sem["xr_saved"], 16)

            def load_x1(b):
                sp.wait_ge(sem["acc_saved"], 16 * b)
                sp.sem_inc(sem["settled_sp"], 1)
                sp.wait_ge(sem["xr_saved"], 16 * b + 16)
                sp.sem_inc(sem["settled_sp"], 1)
                sp.dma_start(x1[:, :], image_acc(b)).then_inc(sem["x1_loaded"], 16)

            def save_acc(b):
                sp.wait_ge(sem["acc_done"], 2 * b + 2)
                sp.sem_inc(sem["settled_sp"], 1)
                sp.dma_start(image_acc(b), x1[:, :]).then_inc(sem["acc_saved"], 16)

            def step(b, has1, has2, has3):
                load_x1(b)
                if has1:
                    save_qk(b + 1)
                    stack_qk(b + 1, 0)
                if has2:
                    save_xr(b + 2)
                if has1:
                    stack_qk(b + 1, 1)
                save_acc(b)

            save_xr(0)
            save_qk(0)
            stack_qk(0, 0)
            stack_qk(0, 1)
            save_xr(1)
            images(sp, step)

            def load_taps(c, s):
                for q in range(Q):
                    at = (QD * q + c) * DWK * HANK
                    sp.dma_start(taps[QD * q:QD * q + QD, s, :, QD * q:QD * q + QD],
                                 bass.AP(dw.tensor, at, [[1, QD], [HANK, DWK], [1, QD]])).then_inc(tap_loaded[s], 16)

            sp.wait_ge(sem["tap_zero"], 1)
            for c in range(QD):
                if c >= 4:
                    sp.wait_ge(sem["dw_ready"], c - 3)
                load_taps(c, c % 4)

            for b in range(B):
                sp.wait_ge(sem["out_done"], 2 * b + 2)
                sp.dma_start(out[b].rearrange("c h w -> c (h w)"), acc[b]).then_inc(sem["stored"], 16)
            sp.wait_ge(sem["stored"], 16 * B)

        @block.gpsimd
        def _(pool):
            pool.memset(power[:, 0, :], -0.5)
            pool.memset(power[:, 1, :], 0.5)
            pool.memset(xn[:, :, :], 0.0)
            pool.memset(ct[:, :], 0.0)
            pool.memset(vp[:, :, :, :], 0.0).then_inc(sem["setup_pool"], 1)
            pool.wait_ge(sem["setup_pool"], 1)
            pool.wait_ge(sem["setup_dve"], 8)
            nc.gpsimd.tensor_tensor(srs[:, 0:B], sva[:, :], power[:, 0, 0:B], ALU.pow)
            nc.gpsimd.tensor_tensor(srs[:, B:2 * B], ssq[:, :], power[:, 1, 0:B], ALU.pow).then_inc(sem["setup_pool"], 1)
            pool.wait_ge(sem["setup_dve"], 3)
            rows = vt[:, :].rearrange("p (s y) -> p s y", y=HP)
            pool.memset(rows[:, :, 0:PAD], 0.0)
            pool.memset(rows[:, :, HP - PAD:HP], 0.0).then_inc(sem["vt_clear"], 1)

            def choose(j):
                if isinstance(j, int) and j == 0:
                    pool.wait_ge(sem["setup_dve"], 31)
                    pool.wait_ge(sem["setup_pool"], 2)
                else:
                    pool.wait_ge(sem["g_ready"], conv_use(j - 1) + G_CONV)
                    pool.wait_ge(sem["coefs_done"], j)
                pool.sem_inc(sem["settled_pool"], 1)
                nc.gpsimd.tensor_copy(gb[:, 0, 0:1], w[:, SHG:SHG + 1])
                nc.gpsimd.tensor_copy(gb[:, 1, 0:1], w[:, SHB:SHB + 1])
                for k in range(TOP):
                    e = pool.value_load(rnum[0:1, bass.ds(4 * j + 2 + k, 1)], min_val=0, max_val=E - 1)
                    pool.dma_start(wsel[:, k, :], wx[bass.ds(e, 1)].rearrange("e p n -> p (e n)")
                                   ).then_inc(sem["chosen_w"], 16)
                    nc.gpsimd.tensor_copy(gb[:, 0, 1 + k:2 + k], w[:, bass.ds(e + EXG, 1)])
                    last = nc.gpsimd.tensor_copy(gb[:, 1, 1 + k:2 + k], w[:, bass.ds(e + EXB, 1)])
                last.then_inc(sem["chosen"], 1)

            def load_x(j):
                if not (isinstance(j, int) and j == 0):
                    pool.wait_ge(sem["sum_shared"], j)
                    pool.sem_inc(sem["settled_pool"], 1)
                src = x[j] if isinstance(j, int) else x[bass.ds(j, 1)]
                src = src.rearrange("c h w -> c (h w)") if isinstance(j, int) else src.rearrange("b c h w -> c (b h w)")
                pool.dma_start(xin[:, :], src).then_inc(sem["xin_loaded"], 16)

            def load_rows(j):
                pool.wait_ge(sem["xn_saved"], 16 * j + 16)
                pool.sem_inc(sem["settled_pool"], 1)
                for k in range(TOP):
                    e = pool.value_load(rnum[0:1, bass.ds(4 * j + 2 + k, 1)], min_val=0, max_val=E - 1)
                    size = (H + 2) * WPAD
                    for s in range(2):
                        src = bass.AP(xs.tensor, e * (GC * size) + s * WPAD, [[1, 3], [size, GC], [1, RUN]])
                        dst = xsh[SH // 2 * s:SH // 2 * (s + 1), k, :, :].rearrange("p h w -> p (h w)")[:, 0:RUN]
                        pool.dma_start(dst, src).then_inc(sem["rows_loaded"], 16)

            def rsqrt(j, n, count):
                pool.wait_ge(sem["group_var"], 2 * j + n + 1)
                nc.gpsimd.tensor_tensor(rstd[:, 0:count], var[:, 0:count], power[:, 0, 0:count],
                                        ALU.pow).then_inc(sem["rstd_done"], 1)

            def step(b, has1, has2, has3):
                pool.wait_ge(sem["v_turned"], b + 1)
                pool.sem_inc(sem["settled_pool"], 1)
                src = vtmp[:, :].rearrange("p (c y) -> p c y", c=QD)
                dst = vt[:, :].rearrange("p (c s) -> p c s", c=QD)[:, :, bass.ds(b * HP + PAD, H)]
                nc.gpsimd.tensor_copy(dst, src).then_inc(sem["vt_done"], 1)
                if has2:
                    rsqrt(b + 2, 0, 3)
                if has3:
                    choose(b + 3)
                    load_x(b + 3)
                if has3:
                    load_rows(b + 3)
                if has2:
                    rsqrt(b + 2, 1, 1)

            load_x(0)
            choose(0)
            load_rows(0)
            rsqrt(0, 0, 3)
            choose(1)
            load_x(1)
            rsqrt(0, 1, 1)
            load_rows(1)
            rsqrt(1, 0, 3)
            choose(2)
            load_x(2)
            rsqrt(1, 1, 1)
            load_rows(2)
            pool.wait_ge(sem["vt_clear"], 1)
            images(pool, step)

            pool.wait_ge(sem["st_ready"], B * PAIRS)
            pool.memset(stack[:, 0:4 * DWK * C], 0.0).then_inc(sem["tap_zero"], 1)

        @block.scalar
        def _(act):
            act.wait_ge(sem["setup_pe"], 1)
            act.activation(hb[:, 0:TABLE // 2], tbk[0][:, 0:TABLE // 2], ACT.Silu, scale=BN)
            act.activation(hb[:, TABLE // 2:], sbk[0][:, 0:TABLE // 2], ACT.Silu, scale=BN).then_inc(sem["setup_act"], 1)
            act.wait_ge(sem["setup_pe"], 2)
            act.activation(xw[:, 0:512], tbk[1][:, :], ACT.Sigmoid, scale=BN).then_inc(sem["setup_act"], 1)
            for n in range(2):
                act.wait_ge(sem["setup_dve"], (14, 19)[n])
                act.activation(rs[:, 8:16], rs[:, 0:8], ACT.Exp, bias=rs[:, 16:17],
                               accum_out=rs[:, 17:18]).then_inc(sem["setup_act"], 1)

            def normalise(j):
                act.wait_ge(sem["xin_loaded"], 16 * j + 16)
                if isinstance(j, int) and j == 0:
                    act.wait_ge(sem["setup_dve"], 9)
                    act.wait_ge(sem["setup_pool"], 1)
                    sc, sh = gn0[:, 0, 0:1], gn0[:, 1, 0:1]
                else:
                    act.wait_ge(sem["xn_saved"], 16 * j)
                    act.wait_ge(sem["g_ready"], conv_use(j - 1) + G_CONV)
                    sc, sh = gn0[:, 0, bass.ds(j, 1)], gn0[:, 1, bass.ds(j, 1)]
                act.activation(xn[:, 1:H + 1, 1:W + 1], xin[:, :].rearrange("p (y x) -> p y x", x=W), ACT.Identity, bias=sh, scale=sc).then_inc(sem["xn_done"], 1)
                act.wait_ge(sem["xn_done"], j + 1)
                if not (isinstance(j, int) and j == 0):
                    act.wait_ge(sem["rows_loaded"], 32 * TOP * j)
                act.dma_start(xs, xn[:, :, :].rearrange("p h w -> p (h w)")).then_inc(sem["xn_saved"], 16)

            def copy_y(j, k):
                u = conv_use(j)
                if k == 0:
                    if isinstance(j, int) and j == 0:
                        act.wait_ge(sem["setup_dve"], 33)
                    else:
                        act.wait_ge(sem["xr_done"], j)
                for h in range(2):
                    act.wait_ge(sem["g_ready"], u + 2 * k + h + 1)
                    act.activation(y[:, k, h * HALF:(h + 1) * HALF], g[h][:, :],
                                   ACT.Identity).then_inc(sem["y_copied"], 1)

            def silu(j):
                act.wait_ge(sem["coefs_done"], j + 1)
                for k in range(3):
                    act.activation(y[:, k, :], y[:, k, :], ACT.Silu, bias=coef[:, 1, k:k + 1],
                                   scale=coef[:, 0, k:k + 1]).then_inc(sem["silu_done"], 1)

            def window(j):
                act.wait_ge(sem["coef_shift"], 2 * j + 2)
                if not (isinstance(j, int) and j == 0):
                    act.wait_ge(sem["g_ready"], qkv_use(j - 1) + G_QKV)
                else:
                    act.wait_ge(sem["setup_dve"], 33)
                src = xr[:, :].rearrange("p (wy r wx c) -> p wy r wx c", wy=ROWS, r=WS, wx=ROWS)
                dst = xw[:, :].rearrange("p (wy wx r c) -> p wy r wx c", wy=ROWS, r=WS, wx=ROWS)
                for wy in range(ROWS):
                    last = act.activation(dst[:, wy], src[:, wy], ACT.Identity, bias=coef2[:, 1:2],
                                          scale=coef2[:, 0:1])
                last.then_inc(sem["xw_done"], 1)

            def high_qk(b, n):
                dst, col, used, each, hi = ((qhl, BQ, "q_saved", 16, "q_hi"), (khl, BK, "k_split", 1, "k_hi"))[n]
                act.wait_ge(sem[used], each * b)
                for h in range(2):
                    act.wait_ge(sem["g_ready"], qkv_use(b) + 2 * n + h + 1)
                    act.activation(dst[:, 0, h * HALF:(h + 1) * HALF], g[h][:, :], ACT.Identity,
                                   bias=w[:, col:col + 1]).then_inc(sem[hi], 1)

            def part_k(b):
                act.wait_ge(sem["k_hi"], 2 * b + 2)
                act.wait_ge(sem["k_saved"], 16 * b)
                for par in range(2):
                    last = act.activation(kpar[:, 0, :, par, :], khl[:, 0, :].rearrange("p (w m) -> p w m", m=TOK),
                                          ACT.Identity, scale=cc[:, PM + par:PM + par + 1])
                last.then_inc(sem["k_split_hi"], 1)

            def v_out(b):
                u = qkv_use(b)
                act.wait_ge(sem["v_turned"], b)
                for h in range(2):
                    act.wait_ge(sem["g_ready"], u + 4 + h + 1)
                    act.activation(vn[:, h * HALF:(h + 1) * HALF], g[h][:, :], ACT.Identity,
                                   bias=w[:, BV:BV + 1]).then_inc(sem["v_done"], 1)
                act.wait_ge(sem["pv_done"], PAIRS * b)
                for h in range(2):
                    act.wait_ge(sem["g_ready"], u + 6 + h + 1)
                    for par in range(2):
                        rows = slice(TOK * par, TOK * par + TOK)
                        act.activation(vp[rows, PAIRS * h:PAIRS * (h + 1), :, HD * par:HD * par + HD],
                                       g[h][rows, :].rearrange("p (w i c) -> p w i c", w=PAIRS, i=Q),
                                       ACT.Identity).then_inc(sem["vp_done"], 1)

            def exponential(b, p):
                s = PAIRS * b + p
                act.wait_ge(sem["st_ready"], s + 1)
                act.wait_ge(sem["pv_done"], PAIRS * b + max(p - 1, 0))
                act.activation(pt[:, p % 2].rearrange("p w i n -> p (w i n)"), tbk[p % 2][:, :],
                               ACT.Exp).then_inc(sem["exp_done"], 1)

            def step(b, has1, has2, has3):
                if has2:
                    copy_y(b + 2, 0)
                for p in range(PAIRS):
                    if has2 and p == P_Y + 1:
                        silu(b + 2)
                    exponential(b, p)
                    if has1 and p in (P_QK, P_QK + 1):
                        high_qk(b + 1, p - P_QK)
                    if has1 and p == P_QK + 1:
                        part_k(b + 1)
                    if has1 and p == 0:
                        window(b + 1)
                    if has2 and p < TOP:
                        copy_y(b + 2, p + 1)
                if has3:
                    normalise(b + 3)
                if has1:
                    v_out(b + 1)

            normalise(0)
            for k in range(3):
                copy_y(0, k)
            silu(0)
            normalise(1)
            window(0)
            high_qk(0, 0)
            high_qk(0, 1)
            part_k(0)
            v_out(0)
            for k in range(3):
                copy_y(1, k)
            silu(1)
            normalise(2)
            images(act, step)

            act.wait_ge(sem["acc_saved"], 16 * B)
            for c in range(QD):
                if c % 2 == 0:
                    act.dma_start(acc[c // 2], acc_d[c // 2]).then_inc(sem["acc_loaded"], 16)
                act.wait_ge(sem["dw_ready"], c + 1)
                src = (sbk + tbk)[c % 4]
                act.activation(vt[:, c * SLOT:c * SLOT + 512], src[:, :], ACT.Identity).then_inc(sem["dw_copied"], 1)

        @block.vector
        def _(dve):
            v = nc.vector
            step_no = [0]

            def link(ins):
                step_no[0] += 1
                ins.then_inc(sem["setup_dve"], 1)
                dve.wait_ge(sem["setup_dve"], step_no[0])

            dve.wait_ge(sem["w_loaded"], 64)
            link(v.tensor_copy(sel[:, :], tc[:, SEL:SEL + Q * C]))
            link(v.tensor_copy(ident2[:, :], tc[:, ID2:ID2 + C]))
            for b in range(B):
                dve.wait_ge(x_loaded[b // 4], 16)
                v.bn_stats(sst[:, 2 * b, :], xall[:, b, 0:HALF])
                last = v.bn_stats(sst[:, 2 * b + 1, :], xall[:, b, HALF:PIX])
            link(last)
            for b in range(B):
                last = v.bn_aggr(smv[:, b, :], sst[:, 2 * b:2 * b + 2, :].rearrange("p a s -> p (a s)"))
            link(last)
            link(v.tensor_tensor(ssq[:, :], smv[:, :, 0], smv[:, :, 0], ALU.mult))
            link(v.tensor_tensor(sgs[:, :, 1], smv[:, :, 1], ssq[:, :], ALU.add))
            v.tensor_scalar(ssq[:, :], smv[:, :, 1], PIX / (PIX - 1.0), None, ALU.mult)
            link(v.tensor_copy(sgs[:, :, 0], smv[:, :, 0]))
            dve.wait_ge(sem["sm_ready"], 1)
            v.tensor_copy(sgs[:, :, :].rearrange("p b t -> p (b t)"), sm[:, 0:2 * B]).then_inc(sem["setup_read"], 1)
            dve.wait_ge(sem["setup_read"], 1)
            v.tensor_tensor(sva[:, :], sgs[:, :, 0], sgs[:, :, 0], ALU.mult).then_inc(sem["group_square"], 1)
            dve.wait_ge(sem["group_square"], 1)
            link(v.scalar_tensor_tensor(out=sva[:, :], in0=sgs[:, :, 1], scalar=EPS, in1=sva[:, :],
                                        op0=ALU.add, op1=ALU.subtract))
            dve.wait_ge(sem["setup_pool"], 2)
            v.tensor_copy(gn0[:, 0, :], srs[:, 0:B])
            link(v.scalar_tensor_tensor(out=gn0[:, 1, :], in0=sgs[:, :, 0], scalar=-1.0, in1=srs[:, 0:B],
                                        op0=ALU.mult, op1=ALU.mult))
            link(v.tensor_tensor(sva[:, :], smv[:, :, 0], sgs[:, :, 0], ALU.subtract))
            v.tensor_tensor(smv[:, :, 0], sva[:, :], srs[:, 0:B], ALU.mult)
            link(v.tensor_tensor(smv[:, :, 1], srs[:, B:2 * B], srs[:, 0:B], ALU.mult))
            dve.wait_ge(sem["sm_ready"], 2)
            v.tensor_copy(rs[:, 0:8], sm[0:B, 0:E]).then_inc(sem["setup_read"], 1)
            dve.wait_ge(sem["setup_read"], 2)
            link(v.tensor_copy(rs[:, 40:48], rs[:, 0:8]))
            for n in range(2):
                if n:
                    link(v.tensor_scalar(rs[:, 0:8], rs[:, 24:32], 30.0, -30.0, ALU.min, ALU.max))
                link(v.tensor_reduce(rs[:, 18:19], rs[:, 0:8], AX.X, ALU.max))
                link(v.tensor_scalar(rs[:, 16:17], rs[:, 18:19], -1.0, None, ALU.mult))
                dve.wait_ge(sem["setup_act"], 3 + n)
                link(v.reciprocal(rs[:, 19:20], rs[:, 17:18]))
                link(v.tensor_scalar(rs[:, 24:32], rs[:, 8:16], rs[:, 19:20], None, ALU.mult))
            link(v.max(rs[:, 32:40], rs[:, 24:32]))
            link(v.max_index(ri[:, :], rs[:, 32:40], rs[:, 24:32]))
            link(v.tensor_tensor(rs[:, 20:21], rs[:, 32:33], rs[:, 33:34], ALU.add))
            link(v.tensor_scalar(rs[:, 21:22], rs[:, 20:21], 1e-6, None, ALU.add))
            link(v.reciprocal(rs[:, 22:23], rs[:, 21:22]))
            v.tensor_scalar(rs[:, 48:50], rs[:, 32:34], rs[:, 22:23], None, ALU.mult)
            link(v.tensor_copy(rs[:, 50:52], ri[:, 0:2]))
            for b in range(B):
                last = v.tensor_scalar(rb[:, b, :], rs[:, 48:52], tc[0:B, EYE + b:EYE + b + 1], None, ALU.mult)
            link(last)
            dve.wait_ge(sem["sm_ready"], 3)
            v.tensor_copy(route[:, :, :].rearrange("p b t -> p (b t)"), sm[:, 0:4 * B]).then_inc(sem["setup_read"], 1)
            dve.wait_ge(sem["setup_read"], 3)
            link(v.tensor_copy(identb[:, :], tc[:, ID:ID + C]))
            link(v.tensor_scalar(w[:, WQ:WQ + C], w[:, WQ:WQ + C], HD ** -0.5, None, ALU.mult))
            link(v.tensor_copy(rnum[:, :], route[0:1, :, :].rearrange("p b t -> p (b t)")))
            dve.wait_ge(sem["setup_act"], 2)
            src = xw[:, 0:512].rearrange("p (m h) -> p h m", h=HEADS)
            dst = bias[:, :].rearrange("p (h m) -> p h m", h=HEADS)
            link(v.tensor_scalar(dst, src, 16.0, None, ALU.mult))
            link(v.scalar_tensor_tensor(out=dst[TOK:C], in0=src[TOK:C], scalar=16.0, in1=dst[TOK:C],
                                        op0=ALU.mult, op1=ALU.subtract))
            dve.wait_ge(sem["sm_ready"], 4)
            v.tensor_tensor(btot[:, :], sm[:, 0:1], w[:, BP:BP + 1], ALU.add).then_inc(sem["setup_read"], 1)
            dve.wait_ge(sem["setup_read"], 4)
            link(v.tensor_scalar(w[:, BQ:BQ + 1], w[:, BQ:BQ + 1], HD ** -0.5, None, ALU.mult))

            def group_sums(j, n, count):
                v.tensor_tensor(sq[:, 0:count], mv[:, 0:count, 0], mv[:, 0:count, 0],
                                ALU.mult).then_inc(sem["squares_done"], 1)
                dve.wait_ge(sem["squares_done"], 2 * j + n + 1)
                v.tensor_tensor(mv[:, 0:count, 1], mv[:, 0:count, 1], sq[:, 0:count],
                                ALU.add).then_inc(sem["sums_done"], 1)

            def group_variance(j, n, count, use):
                dve.wait_ge(sem["sm_ready"], use)
                v.tensor_copy(gs[:, 0:count, :].rearrange("p k t -> p (k t)"),
                              sm[:, 0:2 * count]).then_inc(sem["group_read"], 1)
                dve.wait_ge(sem["group_read"], 2 * j + n + 1)
                v.tensor_tensor(sq[:, 0:count], gs[:, 0:count, 0], gs[:, 0:count, 0],
                                ALU.mult).then_inc(sem["group_square"], 1)
                dve.wait_ge(sem["group_square"], 2 * j + n + 2)
                v.scalar_tensor_tensor(out=var[:, 0:count], in0=gs[:, 0:count, 1], scalar=EPS,
                                       in1=sq[:, 0:count], op0=ALU.add,
                                       op1=ALU.subtract).then_inc(sem["group_var"], 1)

            def y_stats(j, k):
                for h in range(2):
                    dve.wait_ge(sem["y_copied"], 6 * j + 2 * k + h + 1)
                    last = v.bn_stats(st[:, 2 * k + h, :], y[:, k, h * HALF:(h + 1) * HALF])
                if k == 2:
                    last.then_inc(sem["bn_done"], 1)
                    dve.wait_ge(sem["bn_done"], 2 * j + 1)
                    dve.sem_inc(sem["settled_dve"], 1)
                    for k in range(3):
                        last = v.bn_aggr(mv[:, k, :], st[:, 2 * k:2 * k + 2, :].rearrange("p a s -> p (a s)"))
                    last.then_inc(sem["aggr_done"], 1)
                    dve.wait_ge(sem["aggr_done"], 2 * j + 1)
                    group_sums(j, 0, 3)

            def y_coefs(j):
                dve.wait_ge(sem["rstd_done"], 2 * j + 1)
                dve.wait_ge(sem["chosen"], j + 1)
                if not (isinstance(j, int) and j == 0):
                    dve.wait_ge(sem["silu_done"], 3 * j)
                v.tensor_tensor(coef[:, 0, :], rstd[:, :], gb[:, 0, :], ALU.mult).then_inc(sem["coef_scale"], 1)
                dve.wait_ge(sem["coef_scale"], 2 * j + 1)
                v.tensor_tensor(shift[:, :], gs[:, :, 0], coef[:, 0, :], ALU.mult).then_inc(sem["coef_shift"], 1)
                dve.wait_ge(sem["coef_shift"], 2 * j + 1)
                v.tensor_tensor(coef[:, 1, :], gb[:, 1, :], shift[:, :], ALU.subtract).then_inc(sem["coefs_done"], 1)

            def residual(j, part):
                wk = [(route[:, j, k:k + 1] if isinstance(j, int)
                       else route[:, :, :].rearrange("p b t -> p (b t)")[:, bass.ds(4 * j + k, 1)]) for k in range(TOP)]
                if part == 0:
                    dve.wait_ge(sem["silu_done"], 3 * j + 1)
                    if not (isinstance(j, int) and j == 0):
                        dve.wait_ge(sem["xr_saved"], 16 * j)
                        dve.wait_ge(sem["xw_done"], j)
                    v.tensor_tensor(xr[:, :], y[:, 0, :], xin[:, :], ALU.add).then_inc(sem["sum_shared"], 1)
                    return
                if part == 1:
                    dve.wait_ge(sem["silu_done"], 3 * j + 2)
                    dve.wait_ge(sem["sum_shared"], j + 1)
                    v.scalar_tensor_tensor(out=xr[:, :], in0=y[:, 1, :], scalar=wk[0], in1=xr[:, :],
                                           op0=ALU.mult, op1=ALU.add).then_inc(sem["sum_first"], 1)
                    return
                dve.wait_ge(sem["silu_done"], 3 * j + 3)
                dve.wait_ge(sem["sum_first"], j + 1)
                v.scalar_tensor_tensor(out=xr[:, :], in0=y[:, 2, :], scalar=wk[1], in1=xr[:, :],
                                       op0=ALU.mult, op1=ALU.add).then_inc(sem["xr_done"], 1)
                dve.wait_ge(sem["xr_done"], j + 1)
                for h in range(2):
                    last = v.bn_stats(st[:, h, :], xr[:, h * HALF:(h + 1) * HALF])
                last.then_inc(sem["bn_done"], 1)
                dve.wait_ge(sem["bn_done"], 2 * j + 2)
                dve.sem_inc(sem["settled_dve"], 1)
                v.bn_aggr(mv[:, 0, :], st[:, 0:2, :].rearrange("p a s -> p (a s)")).then_inc(sem["aggr_done"], 1)
                dve.wait_ge(sem["aggr_done"], 2 * j + 2)
                group_sums(j, 1, 1)

            def x_coefs(j):
                dve.wait_ge(sem["rstd_done"], 2 * j + 2)
                v.tensor_copy(coef2[:, 0:1], rstd[:, 0:1]).then_inc(sem["coef_scale"], 1)
                v.scalar_tensor_tensor(out=coef2[:, 1:2], in0=gs[:, 0, 0:1], scalar=-1.0, in1=rstd[:, 0:1],
                                       op0=ALU.mult, op1=ALU.mult).then_inc(sem["coef_shift"], 1)

            def maxima(b, p):
                s = PAIRS * b + p
                dve.wait_ge(sem["s_ready"], s + 1)
                v.tensor_reduce(mx[:, :], sbk[p % 2][:, :].rearrange("p (h m) -> p h m", h=HEADS), AX.X,
                                ALU.max).then_inc(sem["s_max"], 1)
                dve.wait_ge(sem["s_max"], s + 1)
                v.tensor_copy(cm[:, 0:HEADS], mx[:, :]).then_inc(sem["c_hi"], 1)
                dve.wait_ge(sem["c_hi"], s + 1)
                v.tensor_tensor(cm[:, HEADS:2 * HEADS], mx[:, :], cm[:, 0:HEADS], ALU.subtract).then_inc(sem["c_lo"], 1)

            def outputs(b, r):
                n = ROWS * b + r
                dve.wait_ge(sem["pv_done"], PAIRS * b + 2 * r + 2)
                v.reciprocal(rec[:, :], pvb[:, WROW:2 * WROW]).then_inc(sem["recip_done"], 1)
                dve.wait_ge(sem["recip_done"], n + 1)
                if r == 0 and not (isinstance(b, int) and b == 0):
                    dve.wait_ge(sem["acc_done"], 2 * b)
                v.tensor_tensor(o[:, r * WROW:(r + 1) * WROW].rearrange("p (r x c) -> p x r c", r=WS, x=ROWS),
                                pvb[:, 0:WROW].rearrange("p (x r c) -> p x r c", r=WS, x=ROWS),
                                rec[:, :].rearrange("p (x r c) -> p x r c", r=WS, x=ROWS),
                                ALU.mult).then_inc(sem["o_done"], 1)

            def low_qk(b, n):
                dst, col, hi, lo = ((qhl, BQ, "q_hi", "q_lo"), (khl, BK, "k_hi", "k_lo"))[n]
                for h in range(2):
                    part = slice(h * HALF, (h + 1) * HALF)
                    dve.wait_ge(sem[hi], 2 * b + h + 1)
                    v.scalar_tensor_tensor(out=dst[:, 1, part], in0=g[h][:, :], scalar=w[:, col:col + 1],
                                           in1=dst[:, 0, part], op0=ALU.add, op1=ALU.subtract
                                           ).then_inc(sem[lo], 1)

            def part_k(b):
                dve.wait_ge(sem["k_lo"], 2 * b + 2)
                dve.wait_ge(sem["k_saved"], 16 * b)
                for par in range(2):
                    last = v.tensor_scalar(kpar[:, 1, :, par, :], khl[:, 1, :].rearrange("p (w m) -> p w m", m=TOK),
                                           cc[:, PM + par:PM + par + 1], None, ALU.mult)
                last.then_inc(sem["k_split"], 1)

            def turn_v(b):
                dve.wait_ge(sem["v_done"], 2 * b + 2)
                dve.wait_ge(sem["vt_done"], b)
                v.transpose(vtmp[:, :].rearrange("p (c y) -> p y c", c=QD),
                            vn[:, :].rearrange("p (y x) -> p y x", x=W)[:, :, ::-1]).then_inc(sem["v_turned"], 1)

            def step(b, has1, has2, has3):
                for p in range(PAIRS):
                    s = PAIRS * b + p
                    dve.wait_ge(sem["sm_ready"], sm_use(b, f"max{p}"))
                    dve.wait_ge(sem["st_ready"], s)
                    v.tensor_copy(ct[0:2 * HEADS, :], smb[0:2 * HEADS, 0:C]).then_inc(sem["ct_done"], 1)
                    if p < PAIRS - 1:
                        maxima(b, p + 1)
                    if p % 2 == 0 and p:
                        outputs(b, p // 2 - 1)
                    if has2 and p == P_Y:
                        group_variance(b + 2, 0, 3, sm_use(b, "gn_y"))
                    if has1 and p in (P_QK, P_QK + 1):
                        low_qk(b + 1, p - P_QK)
                    if has2 and p == P_Y:
                        y_coefs(b + 2)
                    if has2 and p <= TOP:
                        y_stats(b + 2, p)
                    if has1 and p == P_QK + 2:
                        part_k(b + 1)
                    if has2 and p >= P_X:
                        residual(b + 2, p - P_X)
                if has1:
                    maxima(b + 1, 0)
                outputs(b, ROWS - 1)
                if has2:
                    group_variance(b + 2, 1, 1, sm_use(b, "gn_x"))
                u = proj_use(b)
                for h in range(2):
                    dve.wait_ge(sem["g_ready"], u + h + 1)
                    dve.wait_ge(sem["x1_loaded"], 16 * b + 16)
                    part = slice(h * HALF, (h + 1) * HALF)
                    v.scalar_tensor_tensor(out=x1[:, part], in0=g[h][:, :], scalar=btot[:, 0:1], in1=x1[:, part],
                                           op0=ALU.add, op1=ALU.add).then_inc(sem["acc_done"], 1)
                if has1:
                    turn_v(b + 1)
                if has2:
                    x_coefs(b + 2)

            for k in range(3):
                y_stats(0, k)
            group_variance(0, 0, 3, SM_SETUP + 1)
            y_coefs(0)
            residual(0, 0)
            residual(0, 1)
            residual(0, 2)
            group_variance(0, 1, 1, SM_SETUP + 2)
            x_coefs(0)
            low_qk(0, 0)
            low_qk(0, 1)
            part_k(0)
            turn_v(0)
            for k in range(3):
                y_stats(1, k)
            group_variance(1, 0, 3, SM_SETUP + 3)
            y_coefs(1)
            residual(1, 0)
            residual(1, 1)
            residual(1, 2)
            group_variance(1, 1, 1, SM_SETUP + 4)
            x_coefs(1)
            maxima(0, 0)
            images(dve, step)

            def turn_back(b):
                dve.wait_ge(sem["dw_copied"], QD)
                if b >= 2:
                    dve.wait_ge(sem["g_ready"], LAST_USE + 2 * (b - 1))
                src = vt[:, :].rearrange("p (c s) -> p s c", c=QD)[:, H * b:H * b + H, :]
                v.transpose((vn, vtmp)[b % 2][:, :].rearrange("p (y x) -> p y x", x=W), src
                            ).then_inc(sem["pe_turned"], 1)

            turn_back(0)
            dve.wait_ge(sem["acc_loaded"], 16 * B)
            for b in range(B):
                if b + 1 < B:
                    turn_back(b + 1)
                for h in range(2):
                    dve.wait_ge(sem["g_ready"], LAST_USE + 2 * b + h + 1)
                    part = slice(h * HALF, (h + 1) * HALF)
                    v.tensor_tensor(acc[b][:, part], g[h][:, :], acc[b][:, part], ALU.add).then_inc(sem["out_done"], 1)

        @block.tensor
        def _(pe):
            mm = nc.tensor.matmul
            pe.wait_ge(sem["w_loaded"], 64)
            for n, bk in enumerate((tbk[0], sbk[0])):
                at = TBL + n * TABLE // 2
                last = mm(bk[:, 0:TABLE // 2], l1s[:, :], tc[0:3, at:at + TABLE // 2], start=True, stop=True)
            last.then_inc(sem["setup_pe"], 1)
            pe.wait_ge(sem["setup_act"], 1)
            for m in range(TOK):
                at = (WS - 1 - m % WS) * REL * WS + (WS - 1 - m // WS) * WS
                for part in range(2):
                    last = mm(tbk[1][TOK * part:TOK * part + TOK, HEADS * m:HEADS * m + HEADS],
                              hb[:, at:at + TOK], w[:, CW2:CW2 + HEADS], start=True, stop=True)
            last.then_inc(sem["setup_pe"], 1)
            pe.wait_ge(sem["setup_dve"], 7)
            mm(sm[:, 0:2 * B], cc[:, AV4:AV4 + C], sgs[:, :, :].rearrange("p b t -> p (b t)"), start=True,
               stop=True).then_inc(sem["sm_ready"], 1)
            pe.wait_ge(sem["setup_dve"], 11)
            mm(sm[0:B, 0:E], smv[:, :, 0], w[:, RWM:RWM + E], start=True, stop=False)
            mm(sm[0:B, 0:E], smv[:, :, 1], w[:, RWS:RWS + E], start=False, stop=True).then_inc(sem["sm_ready"], 1)
            pe.wait_ge(sem["setup_dve"], 28)
            mm(sm[:, 0:4 * B], tc[0:B, ONE:ONE + C], rb[:, :, :].rearrange("p b t -> p (b t)"), start=True,
               stop=True).then_inc(sem["sm_ready"], 1)
            pe.wait_ge(sem["setup_read"], 3)
            mm(sm[:, 0:1], w[:, WP:WP + C], w[:, BV:BV + 1], start=True, stop=True).then_inc(sem["sm_ready"], 1)
            pe.wait_ge(sem["setup_dve"], 34)

            def convolve(j, k):
                first = isinstance(j, int) and j == 0
                if k == 0:
                    pe.wait_ge(sem["xn_done"], j + 1)
                    for h in range(2):
                        if isinstance(j, int) and j == 1:
                            pe.wait_ge(sem["vp_done"], 2 * h + 2)
                        elif isinstance(j, int) and j == 2:
                            pe.wait_ge(sem["y_copied"], G_CONV + 2 * TOP + h + 1)
                        elif not first:
                            pe.wait_ge(sem["acc_done"], 2 * (j - 3) + h + 1)
                        mm(g[h][:, :], w[:, WSH:WSH + C], xn[:, 1 + 16 * h:17 + 16 * h, 1:W + 1], start=True,
                           stop=True).then_inc(sem["g_ready"], 1)
                    return
                if k == 1:
                    pe.wait_ge(sem["rows_loaded"], 32 * TOP * (j + 1))
                    pe.wait_ge(sem["chosen_w"], 16 * TOP * (j + 1))
                for h in range(2):
                    pe.wait_ge(sem["y_copied"], 6 * j + 2 * (k - 1) + h + 1)
                    for dy in range(2):
                        last = mm(g[h][:, :], wsel[:, k - 1, C * dy:C * dy + C],
                                  xsh[:, k - 1, dy + 16 * h:dy + 16 * h + 16, 0:W], start=(dy == 0), stop=(dy == 1))
                    last.then_inc(sem["g_ready"], 1)

            def average(j, n, count, col, maxima=0):
                pe.wait_ge(sem["sums_done"], 2 * j + n + 1)
                if n or not (isinstance(j, int) and j == 0):
                    pe.wait_ge(sem["group_read"], 2 * j + n)
                pe.wait_ge(sem["ct_done"], maxima)
                mm(sm[:, 0:2 * count], cc[:, col:col + C], mv[:, 0:count, :].rearrange("p k t -> p (k t)"),
                   start=True, stop=True).then_inc(sem["sm_ready"], 1)

            def project_qk(b, n):
                if n == 0:
                    pe.wait_ge(sem["xw_done"], b + 1)
                    if isinstance(b, int) and b == B - 1:
                        pe.wait_ge(sem["acc_done"], 2 * (b - 2) + 2)
                    elif isinstance(b, int) and b == 0:
                        pe.wait_ge(sem["y_copied"], G_CONV)
                    else:
                        pe.wait_ge(sem["y_copied"], G_CONV * b + 2 * G_CONV)
                for h in range(2):
                    if n:
                        pe.wait_ge(sem["q_lo"], 2 * b + h + 1)
                    mm(g[h][:, :], w[:, (WQ, WK)[n]:(WQ, WK)[n] + C], xw[:, h * HALF:(h + 1) * HALF], start=True,
                       stop=True).then_inc(sem["g_ready"], 1)

            def project_v(b):
                nat = xw[:, :].rearrange("p (wy wx r c) -> p wy r wx c", wy=ROWS, r=WS, wx=ROWS)
                for h in range(2):
                    pe.wait_ge(sem["k_lo"], 2 * b + h + 1)
                    for k in range(2):
                        last = mm(g[h][:, k * WROW:(k + 1) * WROW], w[:, WV:WV + C], nat[:, 2 * h + k],
                                  start=True, stop=True)
                    last.then_inc(sem["g_ready"], 1)

            def project_vt(b):
                wv = w[:, WV:WV + C].rearrange("p (i t c) -> p t i c", i=Q, t=2)
                for h in range(2):
                    pe.wait_ge(sem["v_done"], 2 * b + h + 1)
                    for n in range(PAIRS):
                        win = PAIRS * h + n
                        for par in range(2):
                            last = mm(g[h][TOK * par:TOK * par + TOK, n * TOK:n * TOK + TOK],
                                      xw[:, win * TOK:win * TOK + TOK], wv[:, par], start=True, stop=True)
                    last.then_inc(sem["g_ready"], 1)

            def scores(b, p):
                s = PAIRS * b + p
                if p == 0:
                    pe.wait_ge(sem["stacked0"], 96 * b + 96)
                if p == PAIRS // 2:
                    pe.wait_ge(sem["stacked1"], 96 * b + 96)
                pe.wait_ge(sem["s_max"], PAIRS * b + max(p - 1, 0))
                bk = sbk[p % 2]
                mm(bk[:, :], ident2[:, :], bias[:, :], start=True, stop=False, skip_group_check=True)
                for i in range(Q):
                    for n in range(2):
                        at = (2 * p + n) * TOK
                        last = mm(bk[TOK * n:TOK * n + TOK, C * i:C * i + C], qs[0:3 * QD, i, at:at + TOK],
                                  ks[0:3 * QD, i, 2 * at:2 * at + C], start=False, stop=(i == Q - 1), skip_group_check=True)
                last.then_inc(sem["s_ready"], 1)

            def turned_scores(b, p):
                s = PAIRS * b + p
                pe.wait_ge(sem["exp_done"], PAIRS * b + max(p - 1, 0))
                bk = tbk[p % 2][:, :].rearrange("p (w i n) -> p i w n", w=2, i=Q)
                for i in range(Q):
                    mm(bk[:, i], bias[:, C * i:C * i + C], ident2[:, :], start=(i == 0), stop=False,
                       skip_group_check=True)
                for i in range(Q):
                    for n in range(2):
                        at = (2 * p + n) * TOK
                        mm(bk[:, i, n], ks[0:3 * QD, i, 2 * at:2 * at + C], qs[0:3 * QD, i, at:at + TOK],
                           start=False, stop=False, skip_group_check=True)
                pe.wait_ge(sem["ct_done"], s + 1)
                for i in range(Q):
                    last = mm(bk[:, i], sel[:, C * i:C * i + C], ct[:, :], start=False, stop=(i == Q - 1),
                              skip_group_check=True)
                last.then_inc(sem["st_ready"], 1)

            def values(b, p):
                s = PAIRS * b + p
                pe.wait_ge(sem["exp_done"], s + 1)
                if p == 0:
                    pe.wait_ge(sem["vp_done"], 4 * b + 4)
                if p % 2 == 0:
                    pe.wait_ge(sem["o_done"], ROWS * b + p // 2)
                at = (p % 2) * 2 * TOK
                for n in range(2):
                    for i in range(Q):
                        mm(pvb[QD * i:QD * i + QD, at + n * TOK:at + n * TOK + TOK], vp[:, 2 * p + n, i, :],
                           pt[:, p % 2, n, i, :], start=True, stop=True)
                for i in range(Q):
                    last = mm(pvb[QD * i:QD * i + QD, WROW + at:WROW + at + 2 * TOK], cc[:, OM:OM + QD],
                              pt[:, p % 2, :, i, :], start=True, stop=True)
                last.then_inc(sem["pv_done"], 1)

            def turn_maxima(b, p, has2):
                pe.wait_ge(sem["c_lo"], PAIRS * b + p + 1)
                pe.wait_ge(sem["ct_done"], PAIRS * b + p)
                pe.wait_ge(sem["group_read"], min(2 * b + 4, 2 * B) if isinstance(b, int) and not has2
                           else 2 * b + 4 + (p > P_Y))
                nc.tensor.transpose(smb[0:2 * HEADS, 0:C], cm[:, :], identb[:, :]).then_inc(sem["sm_ready"], 1)

            def step(b, has1, has2, has3):
                if has2:
                    convolve(b + 2, 0)
                for p in range(PAIRS):
                    if p + 1 < PAIRS:
                        scores(b, p + 1)
                    turn_maxima(b, p, has2)
                    if p:
                        values(b, p - 1)
                    turned_scores(b, p)
                    if has2 and p == P_Y:
                        average(b + 2, 0, 3, AV16, PAIRS * b + p + 1)
                    if has2 and p < TOP:
                        convolve(b + 2, p + 1)
                    if has1 and p in (P_QK, P_QK + 1):
                        project_qk(b + 1, p - P_QK)
                if has1:
                    project_v(b + 1)
                    scores(b + 1, 0)
                values(b, PAIRS - 1)
                if has2:
                    average(b + 2, 1, 1, AV4, PAIRS * (b + 1))
                if has1:
                    project_vt(b + 1)
                pe.wait_ge(sem["o_done"], ROWS * b + ROWS)
                for h in range(2):
                    if has1:
                        pe.wait_ge(sem["vp_done"], 4 * (b + 1) + 2 * h + 2)
                    else:
                        pe.wait_ge(sem["acc_done"], 2 * (B - 2) + h + 1)
                    mm(g[h][:, :], w[:, WP:WP + C], o[:, h * HALF:(h + 1) * HALF], start=True,
                       stop=True).then_inc(sem["g_ready"], 1)

            for k in range(3):
                convolve(0, k)
            average(0, 0, 3, AV16)
            average(0, 1, 1, AV4)
            project_qk(0, 0)
            project_qk(0, 1)
            project_v(0)
            project_vt(0)
            for k in range(3):
                convolve(1, k)
            average(1, 0, 3, AV16)
            average(1, 1, 1, AV4)
            scores(0, 0)
            images(pe, step)

            for c in range(QD):
                pe.wait_ge(tap_loaded[c % 4], 16 * Q * (c // 4 + 1))
                if c >= 4:
                    pe.wait_ge(sem["dw_copied"], c - 3)
                else:
                    pe.wait_ge(sem["vt_done"], B)
                bk = (sbk + tbk)[c % 4]
                for dy in range(DWK):
                    last = mm(bk[:, :], taps[:, c % 4, dy, :], vt4[:, c, :, dy:dy + H], start=(dy == 0),
                              stop=(dy == DWK - 1))
                last.then_inc(sem["dw_ready"], 1)
            for b in range(B):
                pe.wait_ge(sem["pe_turned"], b + 1)
                for h in range(2):
                    if b:
                        pe.wait_ge(sem["out_done"], 2 * (b - 1) + h + 1)
                    else:
                        pe.wait_ge(sem["acc_done"], 2 * (B - 1) + h + 1)
                    mm(g[h][:, :], w[:, WP:WP + C], (vn, vtmp)[b % 2][:, h * HALF:(h + 1) * HALF], start=True,
                       stop=True).then_inc(sem["g_ready"], 1)


def _lay_out(np, a):
    f = np.float32
    g = C // HEADS
    t = np.ascontiguousarray
    qkv = a["L1_conv_qkv_w"]
    shared = np.zeros((C, C), f)
    for n in range(HEADS):
        r = slice(g * n, g * n + g)
        shared[r, r] = a["L0_conv_shared_w"][r, :, 0, 0].T
    rw = a["L0_conv_router_w"]
    cols = [qkv[0:C].T, qkv[C:2 * C].T, qkv[2 * C:].T, a["L1_conv_proj_w"].T, shared, rw[:, 0:C].T, rw[:, C:].T,
            a["L1_conv_cpb_w2"].T, a["L0_conv_expert_g"].T, a["L0_conv_expert_b"].T]
    cols += [v.reshape(C, 1) for v in (a["L0_conv_gn_shared_g"], a["L0_conv_gn_shared_b"], a["L1_conv_qkv_b"][0:C],
                                      a["L1_conv_qkv_b"][C:2 * C], a["L1_conv_qkv_b"][2 * C:], a["L1_conv_proj_b"])]
    wa = t(np.concatenate(cols, axis=1))
    fused = a["L0_conv_fused_w"].reshape(E, C, GC, 3, 3).transpose(0, 3, 4, 2, 1)
    wx = np.zeros((E, 2, 3, GC, 2, C), f)
    wx[:, :, :, :, 0] = fused[:, 0:2]
    wx[:, 1, :, :, 1] = fused[:, 2]
    wx = wx.reshape(E, SH, 2 * C)
    dw = np.zeros((C, DWK, HANK), f)
    dw[:, :, W - 1 - PAD:W + PAD] = a["L1_conv_dw_w"][:, 0, :, ::-1]
    l1 = t(np.concatenate([a["L1_conv_cpb_w1"].T, a["L1_conv_cpb_b1"].reshape(1, C)], axis=0))
    n = np.arange(C)
    cst = np.zeros((C, CCOLS), f)
    cst[:, AV4:AV4 + C] = (n[:, None] // 4 == n[None] // 4) * 0.25
    cst[:, AV16:AV16 + C] = (n[:, None] // 16 == n[None] // 16) * 0.0625
    cst[:, OM:OM + QD] = n[:, None] // TOK == np.arange(QD)[None] // HD
    cst[:, PM:PM + 2] = n[:, None] // HD % 2 == np.arange(2)[None]
    tmp = np.zeros((C, TCOLS), f)
    tmp[:, ID:ID + C] = np.eye(C)
    tmp[:, ID2:ID2 + C] = n[:, None] % TOK == n[None] % TOK
    for r in range(2 * HEADS):
        i, par = (r % HEADS) // 2, r % 2
        tmp[r, SEL + C * i + TOK * par:SEL + C * i + TOK * par + TOK] = -1.0
    tmp[0:B, EYE:EYE + B] = np.eye(B)
    tmp[0:B, ONE:ONE + C] = 1.0
    r = np.arange(-(WS - 1), WS, dtype=f)
    grid = np.stack(np.meshgrid(r, r, indexing="ij"), axis=-1) / (WS - 1) * 8.0
    grid = (np.sign(grid) * np.log2(np.abs(grid) + 1.0) / np.log2(8.0)).astype(f).reshape(-1, 2)
    k = np.arange(TABLE)
    tmp[0:2, TBL:] = grid.T[:, (k // WS % REL) * REL + k // (WS * REL) + k % WS]
    tmp[2, TBL:] = 1.0
    return {"wa": wa, "wx": wx, "dw": dw, "l1": l1, "cst": cst, "tmp": tmp}


def kernel(**inputs):
    import numpy as np
    import concourse.bacc as bacc
    from concourse.bass_utils import run_bass_kernel_spmd as run

    arrays = {"x": np.ascontiguousarray(inputs["x"])}
    arrays.update(_lay_out(np, {k: np.asarray(v) for k, v in inputs.items()}))
    nc = bacc.Bacc("TRN2", target_bir_lowering=False, num_devices=1)
    args = {k: nc.dram_tensor(k, v.shape, mybir.dt.from_np(v.dtype), kind="ExternalInput").ap()
            for k, v in arrays.items()}
    out = nc.dram_tensor("out", (B, C, H, W), F32, kind="ExternalOutput").ap()
    program(nc, args["x"], args["wa"], args["wx"], args["dw"], args["l1"], args["cst"], args["tmp"], out)
    r = run(nc, [arrays], core_ids=[0])
    return r.results[0]["out"]
```

```python
from contextlib import ExitStack

import concourse.bass as bass
from concourse import mybir

F32 = mybir.dt.float32
F16 = mybir.dt.float16
BF16 = mybir.dt.bfloat16
I32 = mybir.dt.int32
U32 = mybir.dt.uint32
ALU = mybir.AluOpType
ACT = mybir.ActivationFunctionType
AX = mybir.AxisListType

B, C, H, W = 16, 128, 32, 32
PIX = H * W
HALF = PIX // 2
E = 8
TOP = 2
QD = 32
Q = C // QD
HEADS, HD = 8, 16
WS = 8
TOK = WS * WS
ROWS = H // WS
WROW = PIX // ROWS
PAIRS = (PIX // TOK) // 2
PAD = 3
HP = H + 2 * PAD
DWK = 7
TAP_RING = 3
HANK = 64
SLOT = B * HP
EPS = 1e-5
BN = float(1.0 / (1.0 + 1e-5) ** 0.5)
REL = 2 * WS - 1
GC = C // E
SH = 2 * 3 * GC
WPAD = W + 2
RUN = H * WPAD + W

WQ, WK, WV, WP, WSH = (C * n for n in range(5))
RWM = 5 * C
RWS = RWM + E
CW2 = RWS + E
EXG = CW2 + HEADS
EXB = EXG + E
VEC = EXB + E
SHG, SHB, BQ, BK, BV, BP = range(VEC, VEC + 6)
WCOLS = VEC + 6
AV4, AV16, OM = 0, C, 2 * C
PM = 2 * C + QD
CCOLS = PM + 2
ID, ID2, SEL, EYE, ONE, TBL = 0, C, 2 * C, 2 * C + 4 * C, 2 * C + 4 * C + B, 2 * C + 4 * C + B + C
TABLE = WS * REL * WS
TCOLS = TBL + TABLE

G_CONV, G_QKV, G_IMAGE = 6, 8, 14
SM_SETUP, SM_IMAGE = 4, PAIRS + 2
P_QK = 2
P_Y = 3
P_SILU = 5
P_X = 5

SEMS = """
w_loaded x_loaded0 x_loaded1 x_loaded2 x_loaded3
setup_dve setup_act setup_pe setup_pool setup_root
xin_loaded xn_saved rows_loaded xn_done chosen chosen_w g_ready
y_copied bn_done aggr_done squares_done sums_done sm_ready setup_read group_read group_square group_var
rstd_done coef_scale coef_shift coefs_done silu_done sum_shared sum_first xr_done
xw_done xr_saved x1_loaded q_hi k_hi q_lo k_lo q_saved k_split k_saved stacked0 stacked1
v_done v_turned v_hi vt_done vt_saved vp_done s_ready s_max c_hi c_lo ct_done st_ready exp_done pv_done
recip_done o_done proj_ready acc_done acc_saved
tap_zero tap_loaded0 tap_loaded1 tap_loaded2 tap_hi tap_lo tap_ready dw_ready dw_copied pe_turned acc_loaded out_done evac_done pool_added stored settled_sp settled_pool settled_dve
""".split()


def program(nc, x, wa, wx, dw, l1, cst, tmp, out):
    with ExitStack() as ctx:
        def sb(name, shape, dt=F32):
            return ctx.enter_context(nc.sbuf_tensor(name, shape, dt))

        def bank(name):
            return ctx.enter_context(nc.psum_tensor(name, [C, 512], F32))

        vt = sb("vt", [C, QD * SLOT])
        vt16 = vt[:, :].bitcast(F16).rearrange("p (i b c y) -> p i b c y", i=2, b=B, c=QD)
        pe_t = vt[:, :].rearrange("p (i b c y) -> p i b c y", i=2, b=B, c=QD)[:, :, :, :, 0:H // 2]
        vst = sb("vst", [C, 2, QD, HP], F16)
        xall = vt[:, 0:B * PIX].rearrange("p (b n) -> p b n", b=B)
        xsh = sb("xsh", [SH, TOP, H + 1, WPAD])
        y = sb("y", [C, 3, PIX])
        tc = y[:, :, :].rearrange("p k n -> p (k n)")
        xin = sb("xin", [C, PIX])
        xn = sb("xn", [C, H + 2, WPAD])
        xr = sb("xr", [C, PIX])
        x1 = sb("x1", [C, PIX])
        xw = sb("xw", [C, PIX])
        vn = sb("vn", [C, PIX])
        vtmp = sb("vtmp", [C, PIX])
        o = sb("o", [C, PIX])
        qhl = sb("qhl", [C, 2, PIX], F16)
        khl = sb("khl", [C, 2, PIX], F16)
        kpar = sb("kpar", [C, 2, 2 * PAIRS, 2, TOK], F16)
        stack = sb("stack", [C, 3 * Q * PIX // 2])
        qs = stack[:, 0:Q * PIX // 2].bitcast(F16).rearrange("p (i n) -> p i n", i=Q)
        ks = stack[:, Q * PIX // 2:].bitcast(F16).rearrange("p (i n) -> p i n", i=Q)
        TAPS = 2 * DWK * 2 * QD
        taps = stack[:, 0:TAP_RING * TAPS].rearrange("p (s n) -> p s n", s=TAP_RING)
        taps16 = stack[:, TAP_RING * TAPS:2 * TAP_RING * TAPS].bitcast(F16).rearrange("p (s t n) -> p s t n", s=TAP_RING, t=2)
        pt = sb("pt", [C, 2, 2, Q, TOK])
        vp = sb("vp", [C, 2 * PAIRS, Q, QD])
        wsel = sb("wsel", [SH, TOP, 2 * C])
        w = sb("w", [C, WCOLS])
        cc = sb("cc", [C, CCOLS])
        bias = sb("bias", [C, Q * C], F16)
        sel = sb("sel", [C, Q * C], BF16)
        ident2 = sb("ident2", [C, C], F16)
        identb = sb("identb", [C, C], BF16)
        rec = sb("rec", [C, WROW])
        gn0 = sb("gn0", [C, 2, B])
        route = sb("route", [C, B, 4])
        rnum = sb("rnum", [1, B * 4], I32)
        st = sb("st", [C, 6, 6])
        mv = sb("mv", [C, 3, 2])
        sq = sb("sq", [C, 3])
        gs = sb("gs", [C, 3, 2])
        var = sb("var", [C, 3])
        rstd = sb("rstd", [C, 3])
        power = sb("power", [C, B])
        gb = sb("gb", [C, 2, 3])
        coef = sb("coef", [C, 2, 3])
        shift = sb("shift", [C, 3])
        coef2 = sb("coef2", [C, 2])
        mx = sb("mx", [C, HEADS])
        cm = sb("cm", [C, 2 * HEADS], BF16)
        ct = sb("ct", [C, C], BF16)
        btot = sb("btot", [C, 1])
        sst = sb("sst", [C, 2 * B, 6])
        smv = sb("smv", [C, B, 2])
        ssq = sb("ssq", [C, B])
        sva = sb("sva", [C, B])
        sgs = sb("sgs", [C, B, 2])
        srs = sb("srs", [C, 3 * B])
        rs = sb("rs", [B, 64])
        rb = sb("rb", [B, B, 4])
        ri = sb("ri", [B, 8], U32)
        l1s = sb("l1s", [3, C])
        hb = o[:, 0:TABLE]
        free = [y[:, n, :] for n in range(3)] + [xin[:, :], xr[:, :], x1[:, :], xw[:, :], o[:, :]]
        free += [t[:, :, :].rearrange("p t n -> p (t n)").bitcast(F32) for t in (qhl, khl)]
        free.append(pt[:, :, :, :, :].rearrange("p s w i n -> p (s w i n)"))
        free.append(xn[:, :, :].rearrange("p h w -> p (h w)")[:, 0:PIX])
        for t in (kpar[:, :, :, :, :].rearrange("p t w a m -> p (t w a m)").bitcast(F32),
                  vp[:, :, :, :].rearrange("p w i c -> p (w i c)")):
            free += [t[:, 0:PIX], t[:, PIX:2 * PIX]]
        acc = free[0:B]
        evac = [stack[:, n * PIX:(n + 1) * PIX] for n in range(2)]

        g = [bank("g0"), bank("g1")]
        sbk = [bank("s0"), bank("s1")]
        tbk = [bank("t0"), bank("t1")]
        pvb = bank("pv")
        sm = bank("sm")
        smb = sm[:, :].bitcast(BF16)

        xs = nc.dram_tensor("xs", [C, (H + 2) * WPAD], F32).ap()
        sq_d = nc.dram_tensor("sq_d", [2, C, PIX], F16).ap()
        sk_d = nc.dram_tensor("sk_d", [2, C, 2 * PIX], F16).ap()
        acc_d = nc.dram_tensor("acc_d", [B, C, PIX], F32).ap()

        sem = {n: ctx.enter_context(nc.semaphore(n)) for n in SEMS}
        tap_loaded = [sem[f"tap_loaded{n}"] for n in range(TAP_RING)]
        stacked = [sem["stacked0"], sem["stacked1"]]
        x_loaded = [sem[f"x_loaded{n}"] for n in range(4)]

        def use_base(b):
            last = isinstance(b, int) and b == B - 1
            return 2 * G_CONV + G_QKV + G_IMAGE * b - (G_CONV if last else 0)

        def conv_use(j):
            if isinstance(j, int) and j < 2:
                return (G_CONV + G_QKV) * j
            return use_base(j - 2)

        def qkv_use(j):
            if isinstance(j, int) and j == 0:
                return G_CONV
            last = isinstance(j, int) and j == B - 1
            return use_base(j - 1) + (0 if last else G_CONV)

        LAST_USE = use_base(B - 1)

        def small_slots(b):
            names = [f"max{p}" for p in range(PAIRS)]
            if not (isinstance(b, int) and b >= B - 2):
                names.insert(P_Y + 1, "gn_y")
                names.append("gn_x")
            return {n: k for k, n in enumerate(names)}

        def sm_use(b, name):
            before = SM_IMAGE * b - (2 if isinstance(b, int) and b == B - 1 else 0)
            return SM_SETUP + 5 + small_slots(b)[name] + before

        def images(eng, step):
            step(0, True, True, True)
            with eng.Fori(1, B - 3) as b:
                step(b, True, True, True)
            step(B - 3, True, True, False)
            step(B - 2, True, False, False)
            step(B - 1, False, False, False)

        block = ctx.enter_context(nc.Block())

        @block.sync
        def _(sp):
            xb = x.rearrange("b c h w -> c b (h w)")
            sp.dma_start(w[:, :], wa).then_inc(sem["w_loaded"], 16)
            sp.dma_start(cc[:, :], cst).then_inc(sem["w_loaded"], 16)
            sp.dma_start(tc[:, 0:TCOLS], tmp).then_inc(sem["w_loaded"], 16)
            sp.dma_start(l1s[:, :], l1).then_inc(sem["w_loaded"], 16)
            for n in range(4):
                sp.dma_start(xall[:, 4 * n:4 * n + 4, :], xb[:, 4 * n:4 * n + 4, :]).then_inc(x_loaded[n], 16)

            def save_qk(j):
                sp.wait_ge(sem["q_lo"], 2 * j + 2)
                sp.sem_inc(sem["settled_sp"], 1)
                if not (isinstance(j, int) and j == 0):
                    sp.wait_ge(sem["stacked1"], 96 * j)
                    sp.sem_inc(sem["settled_sp"], 1)
                sp.dma_start(sq_d.rearrange("t c n -> c t n"), qhl[:, :, :]).then_inc(sem["q_saved"], 16)
                sp.wait_ge(sem["k_split"], j + 1)
                sp.sem_inc(sem["settled_sp"], 1)
                sp.dma_start(sk_d.rearrange("t c n -> c t n"),
                             kpar[:, :, :, :, :].rearrange("p t w a m -> p t (w a m)")).then_inc(sem["k_saved"], 16)

            def stack_qk(j, half):
                if half == 0:
                    sp.wait_ge(sem["q_saved"], 16 * j + 16)
                    sp.sem_inc(sem["settled_sp"], 1)
                    sp.wait_ge(sem["k_saved"], 16 * j + 16)
                    sp.sem_inc(sem["settled_sp"], 1)
                if not (isinstance(j, int) and j == 0):
                    sp.wait_ge(sem["st_ready"], PAIRS * (j - 1) + PAIRS // 2 * (half + 1))
                    sp.sem_inc(sem["settled_sp"], 1)
                n, m = HALF * half, 2 * HALF * half
                for part, t in enumerate((0, 1, 0)):
                    sp.dma_start(qs[QD * part:QD * part + QD, :, n:n + HALF],
                                 sq_d[t, :, n:n + HALF].rearrange("(i c) n -> c i n", i=Q)).then_inc(stacked[half], 16)
                for part, t in enumerate((0, 0, 1)):
                    sp.dma_start(ks[QD * part:QD * part + QD, :, m:m + 2 * HALF],
                                 sk_d[t, :, m:m + 2 * HALF].rearrange("(i c) n -> c i n", i=Q)).then_inc(stacked[half], 16)

            def image_acc(b):
                return acc_d[b] if isinstance(b, int) else acc_d[bass.ds(b, 1)].rearrange("b c n -> c (b n)")

            def save_xr(j):
                sp.wait_ge(sem["xr_done"], j + 1)
                sp.sem_inc(sem["settled_sp"], 1)
                sp.dma_start(image_acc(j), xr[:, :]).then_inc(sem["xr_saved"], 16)

            def load_x1(b):
                sp.wait_ge(sem["acc_saved"], 16 * b)
                sp.sem_inc(sem["settled_sp"], 1)
                sp.wait_ge(sem["xr_saved"], 16 * b + 16)
                sp.sem_inc(sem["settled_sp"], 1)
                sp.dma_start(x1[:, :], image_acc(b)).then_inc(sem["x1_loaded"], 16)

            def place_v(b):
                sp.wait_ge(sem["vt_done"], b + 1)
                sp.sem_inc(sem["settled_sp"], 1)
                images16 = vt[:, :].bitcast(F16).rearrange("p (i n) -> p i n", i=2)
                for part in range(2):
                    for i in range(2):
                        dst = images16[C // 2 * part:C // 2 * (part + 1), i, bass.ds(b * QD * HP, QD * HP)]
                        src = vst[C // 2 * i:C // 2 * (i + 1), part, :, :].rearrange("p c y -> p (c y)")
                        sp.dma_start(dst, src).then_inc(sem["vt_saved"], 16)

            def load_taps(c):
                if c == 0:
                    sp.wait_ge(sem["tap_zero"], 1)
                if c >= TAP_RING:
                    sp.wait_ge(sem["tap_lo"], c - TAP_RING + 1)
                for m in range(2):
                    src = bass.AP(dw.tensor, (QD * m + c) * 2 * DWK * HANK, [[1, QD], [HANK, 2 * DWK], [1, QD]])
                    dst = taps[QD * m:QD * m + QD, c % TAP_RING, :].rearrange("p (r x) -> p r x", x=2 * QD)
                    sp.dma_start(dst[:, :, QD * m:QD * m + QD], src).then_inc(tap_loaded[c % TAP_RING], 16)

            def save_acc(b):
                sp.wait_ge(sem["acc_done"], 2 * b + 2)
                sp.sem_inc(sem["settled_sp"], 1)
                sp.dma_start(image_acc(b), x1[:, :]).then_inc(sem["acc_saved"], 16)

            def step(b, has1, has2, has3):
                place_v(b)
                load_x1(b)
                if has1:
                    save_qk(b + 1)
                    stack_qk(b + 1, 0)
                if has2:
                    save_xr(b + 2)
                if has1:
                    stack_qk(b + 1, 1)
                else:
                    for c in range(TAP_RING):
                        load_taps(c)
                save_acc(b)

            save_xr(0)
            save_qk(0)
            stack_qk(0, 0)
            stack_qk(0, 1)
            save_xr(1)
            images(sp, step)

            for c in range(TAP_RING, QD):
                load_taps(c)

            for b in range(B):
                if b % 2:
                    sp.wait_ge(sem["pool_added"], b // 2 + 1)
                else:
                    sp.wait_ge(sem["out_done"], b + 2)
                sp.dma_start(out[b].rearrange("c h w -> c (h w)"), acc[b]).then_inc(sem["stored"], 16)
            sp.wait_ge(sem["stored"], 16 * B)

        @block.gpsimd
        def _(pool):
            pool.memset(power[:, :], -0.5)
            pool.memset(xn[:, :, :], 0.0)
            pool.memset(ct[:, :], 0.0)
            pool.memset(vst[:, :, :, :], 0.0)
            pool.memset(vp[:, :, :, :], 0.0).then_inc(sem["setup_pool"], 1)

            pool.wait_ge(sem["setup_pool"], 1)
            pool.wait_ge(sem["setup_dve"], 8)
            nc.gpsimd.tensor_tensor(srs[:, 0:B], sva[:, :], power[:, :], ALU.pow).then_inc(sem["setup_pool"], 1)

            def choose(j):
                if isinstance(j, int) and j == 0:
                    pool.wait_ge(sem["setup_dve"], 31)
                    pool.wait_ge(sem["setup_pool"], 1)
                else:
                    pool.wait_ge(sem["g_ready"], conv_use(j - 1) + G_CONV)
                    pool.wait_ge(sem["coefs_done"], j)
                pool.sem_inc(sem["settled_pool"], 1)
                nc.gpsimd.tensor_copy(gb[:, 0, 0:1], w[:, SHG:SHG + 1])
                nc.gpsimd.tensor_copy(gb[:, 1, 0:1], w[:, SHB:SHB + 1])
                for k in range(TOP):
                    e = pool.value_load(rnum[0:1, bass.ds(4 * j + 2 + k, 1)], min_val=0, max_val=E - 1)
                    pool.dma_start(wsel[:, k, :], wx[bass.ds(e, 1)].rearrange("e p n -> p (e n)")
                                   ).then_inc(sem["chosen_w"], 16)
                    nc.gpsimd.tensor_copy(gb[:, 0, 1 + k:2 + k], w[:, bass.ds(e + EXG, 1)])
                    last = nc.gpsimd.tensor_copy(gb[:, 1, 1 + k:2 + k], w[:, bass.ds(e + EXB, 1)])
                last.then_inc(sem["chosen"], 1)

            def load_x(j):
                if not (isinstance(j, int) and j == 0):
                    pool.wait_ge(sem["sum_shared"], j)
                    pool.sem_inc(sem["settled_pool"], 1)
                src = x[j] if isinstance(j, int) else x[bass.ds(j, 1)]
                src = src.rearrange("c h w -> c (h w)") if isinstance(j, int) else src.rearrange("b c h w -> c (b h w)")
                pool.dma_start(xin[:, :], src).then_inc(sem["xin_loaded"], 16)

            def load_rows(j):
                pool.wait_ge(sem["xn_saved"], 16 * j + 16)
                pool.sem_inc(sem["settled_pool"], 1)
                for k in range(TOP):
                    e = pool.value_load(rnum[0:1, bass.ds(4 * j + 2 + k, 1)], min_val=0, max_val=E - 1)
                    size = (H + 2) * WPAD
                    for s in range(2):
                        src = bass.AP(xs.tensor, e * (GC * size) + s * WPAD, [[1, 3], [size, GC], [1, RUN]])
                        dst = xsh[SH // 2 * s:SH // 2 * (s + 1), k, :, :].rearrange("p h w -> p (h w)")[:, 0:RUN]
                        pool.dma_start(dst, src).then_inc(sem["rows_loaded"], 16)

            def rsqrt(j, n, count):
                pool.wait_ge(sem["group_var"], 2 * j + n + 1)
                nc.gpsimd.tensor_tensor(rstd[:, 0:count], var[:, 0:count], power[:, 0:count],
                                        ALU.pow).then_inc(sem["rstd_done"], 1)

            def step(b, has1, has2, has3):
                pool.wait_ge(sem["v_turned"], b + 1)
                pool.sem_inc(sem["settled_pool"], 1)
                pool.wait_ge(sem["vt_saved"], 64 * b)
                pool.sem_inc(sem["settled_pool"], 1)
                src = vtmp[:, :].rearrange("p (c y) -> p c y", c=QD)
                rows = vst[:, :, :, PAD:PAD + H]
                nc.gpsimd.tensor_copy(rows[:, 0], src).then_inc(sem["v_hi"], 1)
                pool.wait_ge(sem["v_hi"], b + 1)
                nc.gpsimd.tensor_tensor(rows[:, 1], src, rows[:, 0], ALU.subtract).then_inc(sem["vt_done"], 1)
                if has2:
                    rsqrt(b + 2, 0, 3)
                if has3:
                    choose(b + 3)
                    load_x(b + 3)
                if has3:
                    load_rows(b + 3)
                if has2:
                    rsqrt(b + 2, 1, 1)

            load_x(0)
            choose(0)
            load_rows(0)
            rsqrt(0, 0, 3)
            choose(1)
            load_x(1)
            rsqrt(0, 1, 1)
            load_rows(1)
            rsqrt(1, 0, 3)
            choose(2)
            load_x(2)
            rsqrt(1, 1, 1)
            load_rows(2)
            images(pool, step)

            pool.wait_ge(sem["st_ready"], B * PAIRS)
            pool.memset(stack[:, 0:TAP_RING * TAPS], 0.0).then_inc(sem["tap_zero"], 1)
            pool.wait_ge(sem["acc_loaded"], 16 * B)
            for n in range(B // 2):
                pool.wait_ge(sem["evac_done"], 2 * n + 2)
                nc.gpsimd.tensor_tensor(acc[2 * n + 1], acc[2 * n + 1], evac[n % 2],
                                        ALU.add).then_inc(sem["pool_added"], 1)

        @block.scalar
        def _(act):
            act.wait_ge(sem["setup_pe"], 1)
            act.activation(hb[:, 0:TABLE // 2], tbk[0][:, 0:TABLE // 2], ACT.Silu, scale=BN)
            act.activation(hb[:, TABLE // 2:], sbk[0][:, 0:TABLE // 2], ACT.Silu, scale=BN).then_inc(sem["setup_act"], 1)
            act.wait_ge(sem["setup_pe"], 2)
            act.activation(xw[:, 0:512], tbk[1][:, :], ACT.Sigmoid, scale=BN).then_inc(sem["setup_act"], 1)
            act.wait_ge(sem["setup_dve"], 8)
            act.activation(srs[:, B:2 * B], ssq[:, :], ACT.Sqrt).then_inc(sem["setup_act"], 1)
            for n in range(2):
                act.wait_ge(sem["setup_dve"], (14, 19)[n])
                act.activation(rs[:, 8:16], rs[:, 0:8], ACT.Exp, bias=rs[:, 16:17],
                               accum_out=rs[:, 17:18]).then_inc(sem["setup_act"], 1)

            def normalise(j):
                act.wait_ge(sem["xin_loaded"], 16 * j + 16)
                if isinstance(j, int) and j == 0:
                    act.wait_ge(sem["setup_dve"], 9)
                    act.wait_ge(sem["setup_pool"], 1)
                    sc, sh = gn0[:, 0, 0:1], gn0[:, 1, 0:1]
                else:
                    act.wait_ge(sem["xn_saved"], 16 * j)
                    act.wait_ge(sem["g_ready"], conv_use(j - 1) + G_CONV)
                    sc, sh = gn0[:, 0, bass.ds(j, 1)], gn0[:, 1, bass.ds(j, 1)]
                act.activation(xn[:, 1:H + 1, 1:W + 1], xin[:, :].rearrange("p (y x) -> p y x", x=W), ACT.Identity, bias=sh, scale=sc).then_inc(sem["xn_done"], 1)
                act.wait_ge(sem["xn_done"], j + 1)
                if not (isinstance(j, int) and j == 0):
                    act.wait_ge(sem["rows_loaded"], 32 * TOP * j)
                act.dma_start(xs, xn[:, :, :].rearrange("p h w -> p (h w)")).then_inc(sem["xn_saved"], 16)

            def copy_y(j, k):
                u = conv_use(j)
                if k == 0:
                    if isinstance(j, int) and j == 0:
                        act.wait_ge(sem["setup_dve"], 33)
                    else:
                        act.wait_ge(sem["xr_done"], j)
                for h in range(2):
                    act.wait_ge(sem["g_ready"], u + 2 * k + h + 1)
                    act.activation(y[:, k, h * HALF:(h + 1) * HALF], g[h][:, :],
                                   ACT.Identity).then_inc(sem["y_copied"], 1)

            def silu(j, k):
                act.wait_ge(sem["coefs_done"], j + 1)
                act.activation(y[:, k, :], y[:, k, :], ACT.Silu, bias=coef[:, 1, k:k + 1],
                               scale=coef[:, 0, k:k + 1]).then_inc(sem["silu_done"], 1)

            def window(j):
                act.wait_ge(sem["coef_shift"], 2 * j + 2)
                if not (isinstance(j, int) and j == 0):
                    act.wait_ge(sem["g_ready"], qkv_use(j - 1) + G_QKV)
                else:
                    act.wait_ge(sem["setup_dve"], 33)
                src = xr[:, :].rearrange("p (wy r wx c) -> p wy r wx c", wy=ROWS, r=WS, wx=ROWS)
                dst = xw[:, :].rearrange("p (wy wx r c) -> p wy r wx c", wy=ROWS, r=WS, wx=ROWS)
                for wy in range(ROWS):
                    last = act.activation(dst[:, wy], src[:, wy], ACT.Identity, bias=coef2[:, 1:2],
                                          scale=coef2[:, 0:1])
                last.then_inc(sem["xw_done"], 1)

            def high_qk(b, n):
                dst, col, used, each, hi = ((qhl, BQ, "q_saved", 16, "q_hi"), (khl, BK, "k_split", 1, "k_hi"))[n]
                act.wait_ge(sem[used], each * b)
                for h in range(2):
                    act.wait_ge(sem["g_ready"], qkv_use(b) + 2 * n + h + 1)
                    act.activation(dst[:, 0, h * HALF:(h + 1) * HALF], g[h][:, :], ACT.Identity,
                                   bias=w[:, col:col + 1]).then_inc(sem[hi], 1)

            def v_out(b):
                u = qkv_use(b)
                act.wait_ge(sem["v_turned"], b)
                for h in range(2):
                    act.wait_ge(sem["g_ready"], u + 4 + h + 1)
                    act.activation(vn[:, h * HALF:(h + 1) * HALF], g[h][:, :], ACT.Identity,
                                   bias=w[:, BV:BV + 1]).then_inc(sem["v_done"], 1)
                act.wait_ge(sem["pv_done"], PAIRS * b)
                for h in range(2):
                    act.wait_ge(sem["g_ready"], u + 6 + h + 1)
                    for par in range(2):
                        rows = slice(TOK * par, TOK * par + TOK)
                        act.activation(vp[rows, PAIRS * h:PAIRS * (h + 1), :, HD * par:HD * par + HD],
                                       g[h][rows, :].rearrange("p (w i c) -> p w i c", w=PAIRS, i=Q),
                                       ACT.Identity).then_inc(sem["vp_done"], 1)

            def exponential(b, p):
                s = PAIRS * b + p
                act.wait_ge(sem["st_ready"], s + 1)
                act.wait_ge(sem["pv_done"], PAIRS * b + max(p - 1, 0))
                act.activation(pt[:, p % 2].rearrange("p w i n -> p (w i n)"), tbk[p % 2][:, :],
                               ACT.Exp).then_inc(sem["exp_done"], 1)

            def step(b, has1, has2, has3):
                if has2:
                    copy_y(b + 2, 0)
                for p in range(PAIRS):
                    if has2 and p == P_SILU:
                        silu(b + 2, 0)
                    if has2 and p == P_SILU + 1:
                        silu(b + 2, 1)
                        silu(b + 2, 2)
                    if has3 and p == PAIRS - 1:
                        normalise(b + 3)
                    exponential(b, p)
                    if has1 and p in (P_QK, P_QK + 1):
                        high_qk(b + 1, p - P_QK)
                    if has1 and p == 0:
                        window(b + 1)
                    if has2 and p < TOP:
                        copy_y(b + 2, p + 1)
                if has1:
                    v_out(b + 1)

            normalise(0)
            for k in range(3):
                copy_y(0, k)
            for k in range(3):
                silu(0, k)
            normalise(1)
            window(0)
            high_qk(0, 0)
            high_qk(0, 1)
            v_out(0)
            for k in range(3):
                copy_y(1, k)
            for k in range(3):
                silu(1, k)
            normalise(2)
            images(act, step)

            def pe_out(c):
                act.wait_ge(sem["dw_ready"], c + 1)
                act.activation(pe_t[:, :, :, c, :], (sbk + tbk)[c % 4][:, :].rearrange("p (b h y) -> p h b y", h=2, b=B),
                               ACT.Identity).then_inc(sem["dw_copied"], 1)

            for c in range(QD):
                if c == 1:
                    act.wait_ge(sem["acc_saved"], 16 * B)
                if c % 2:
                    act.dma_start(acc[c // 2], acc_d[c // 2]).then_inc(sem["acc_loaded"], 16)
                act.wait_ge(tap_loaded[c % TAP_RING], 32 * (c // TAP_RING + 1))
                if c >= TAP_RING:
                    act.wait_ge(sem["dw_ready"], c - TAP_RING + 1)
                act.activation(taps16[0:C // 2, c % TAP_RING, 0, :], taps[0:C // 2, c % TAP_RING, :],
                               ACT.Identity).then_inc(sem["tap_hi"], 1)
                if c:
                    pe_out(c - 1)
            pe_out(QD - 1)
            for n in range(B // 2):
                if n >= 2:
                    act.wait_ge(sem["pool_added"], n - 1)
                for h in range(2):
                    act.wait_ge(sem["g_ready"], LAST_USE + 2 * (2 * n + 1) + h + 1)
                    act.activation(evac[n % 2][:, h * HALF:(h + 1) * HALF], g[h][:, :],
                                   ACT.Identity).then_inc(sem["evac_done"], 1)

        @block.vector
        def _(dve):
            v = nc.vector
            step_no = [0]

            def link(ins):
                step_no[0] += 1
                ins.then_inc(sem["setup_dve"], 1)
                dve.wait_ge(sem["setup_dve"], step_no[0])

            dve.wait_ge(sem["w_loaded"], 64)
            link(v.tensor_copy(sel[:, :], tc[:, SEL:SEL + Q * C]))
            link(v.tensor_copy(ident2[:, :], tc[:, ID2:ID2 + C]))
            for b in range(B):
                dve.wait_ge(x_loaded[b // 4], 16)
                v.bn_stats(sst[:, 2 * b, :], xall[:, b, 0:HALF])
                last = v.bn_stats(sst[:, 2 * b + 1, :], xall[:, b, HALF:PIX])
            link(last)
            for b in range(B):
                last = v.bn_aggr(smv[:, b, :], sst[:, 2 * b:2 * b + 2, :].rearrange("p a s -> p (a s)"))
            link(last)
            link(v.tensor_tensor(ssq[:, :], smv[:, :, 0], smv[:, :, 0], ALU.mult))
            link(v.tensor_tensor(sgs[:, :, 1], smv[:, :, 1], ssq[:, :], ALU.add))
            v.tensor_scalar(ssq[:, :], smv[:, :, 1], PIX / (PIX - 1.0), None, ALU.mult)
            link(v.tensor_copy(sgs[:, :, 0], smv[:, :, 0]))
            dve.wait_ge(sem["sm_ready"], 1)
            v.tensor_copy(sgs[:, :, :].rearrange("p b t -> p (b t)"), sm[:, 0:2 * B]).then_inc(sem["setup_read"], 1)
            dve.wait_ge(sem["setup_read"], 1)
            v.tensor_tensor(sva[:, :], sgs[:, :, 0], sgs[:, :, 0], ALU.mult).then_inc(sem["group_square"], 1)
            dve.wait_ge(sem["group_square"], 1)
            link(v.scalar_tensor_tensor(out=sva[:, :], in0=sgs[:, :, 1], scalar=EPS, in1=sva[:, :],
                                        op0=ALU.add, op1=ALU.subtract))
            dve.wait_ge(sem["setup_act"], 3)
            root, part = srs[:, B:2 * B], srs[:, 2 * B:3 * B]
            for n, ins in enumerate((
                    lambda: v.tensor_scalar(part, root, 1e-30, None, ALU.max),
                    lambda: v.reciprocal(part, part),
                    lambda: v.tensor_tensor(part, part, ssq[:, :], ALU.mult),
                    lambda: v.tensor_tensor(part, part, root, ALU.add),
                    lambda: v.tensor_scalar(root, part, 0.5, None, ALU.mult))):
                ins().then_inc(sem["setup_root"], 1)
                dve.wait_ge(sem["setup_root"], n + 1)
            dve.wait_ge(sem["setup_pool"], 2)
            v.tensor_copy(gn0[:, 0, :], srs[:, 0:B])
            link(v.scalar_tensor_tensor(out=gn0[:, 1, :], in0=sgs[:, :, 0], scalar=-1.0, in1=srs[:, 0:B],
                                        op0=ALU.mult, op1=ALU.mult))
            link(v.tensor_tensor(sva[:, :], smv[:, :, 0], sgs[:, :, 0], ALU.subtract))
            v.tensor_tensor(smv[:, :, 0], sva[:, :], gn0[:, 0, :], ALU.mult)
            link(v.tensor_tensor(smv[:, :, 1], srs[:, B:2 * B], gn0[:, 0, :], ALU.mult))
            dve.wait_ge(sem["sm_ready"], 2)
            v.tensor_copy(rs[:, 0:8], sm[0:B, 0:E]).then_inc(sem["setup_read"], 1)
            dve.wait_ge(sem["setup_read"], 2)
            link(v.tensor_copy(rs[:, 40:48], rs[:, 0:8]))
            for n in range(2):
                if n:
                    link(v.tensor_scalar(rs[:, 0:8], rs[:, 24:32], 30.0, -30.0, ALU.min, ALU.max))
                link(v.tensor_reduce(rs[:, 18:19], rs[:, 0:8], AX.X, ALU.max))
                link(v.tensor_scalar(rs[:, 16:17], rs[:, 18:19], -1.0, None, ALU.mult))
                dve.wait_ge(sem["setup_act"], 4 + n)
                link(v.reciprocal(rs[:, 19:20], rs[:, 17:18]))
                link(v.tensor_scalar(rs[:, 24:32], rs[:, 8:16], rs[:, 19:20], None, ALU.mult))
            link(v.max(rs[:, 32:40], rs[:, 24:32]))
            link(v.max_index(ri[:, :], rs[:, 32:40], rs[:, 24:32]))
            link(v.tensor_tensor(rs[:, 20:21], rs[:, 32:33], rs[:, 33:34], ALU.add))
            link(v.tensor_scalar(rs[:, 21:22], rs[:, 20:21], 1e-6, None, ALU.add))
            link(v.reciprocal(rs[:, 22:23], rs[:, 21:22]))
            v.tensor_scalar(rs[:, 48:50], rs[:, 32:34], rs[:, 22:23], None, ALU.mult)
            link(v.tensor_copy(rs[:, 50:52], ri[:, 0:2]))
            link(v.tensor_tensor(rb[:, :, :], rs[:, 48:52].unsqueeze(1).to_broadcast([B, B, 4]),
                                 tc[0:B, EYE:EYE + B].unsqueeze(2).to_broadcast([B, B, 4]), ALU.mult))
            dve.wait_ge(sem["sm_ready"], 3)
            v.tensor_copy(route[:, :, :].rearrange("p b t -> p (b t)"), sm[:, 0:4 * B]).then_inc(sem["setup_read"], 1)
            dve.wait_ge(sem["setup_read"], 3)
            link(v.tensor_copy(identb[:, :], tc[:, ID:ID + C]))
            link(v.tensor_scalar(w[:, WQ:WQ + C], w[:, WQ:WQ + C], HD ** -0.5, None, ALU.mult))
            link(v.tensor_copy(rnum[:, :], route[0:1, :, :].rearrange("p b t -> p (b t)")))
            dve.wait_ge(sem["setup_act"], 2)
            src = xw[:, 0:512].rearrange("p (m h) -> p h m", h=HEADS)
            dst = bias[:, :].rearrange("p (h m) -> p h m", h=HEADS)
            link(v.tensor_scalar(dst, src, 16.0, None, ALU.mult))
            link(v.scalar_tensor_tensor(out=dst[TOK:C], in0=src[TOK:C], scalar=16.0, in1=dst[TOK:C],
                                        op0=ALU.mult, op1=ALU.subtract))
            dve.wait_ge(sem["sm_ready"], 4)
            v.tensor_tensor(btot[:, :], sm[:, 0:1], w[:, BP:BP + 1], ALU.add).then_inc(sem["setup_read"], 1)
            dve.wait_ge(sem["setup_read"], 4)
            link(v.tensor_scalar(w[:, BQ:BQ + 1], w[:, BQ:BQ + 1], HD ** -0.5, None, ALU.mult))

            def group_sums(j, n, count):
                v.tensor_tensor(sq[:, 0:count], mv[:, 0:count, 0], mv[:, 0:count, 0],
                                ALU.mult).then_inc(sem["squares_done"], 1)
                dve.wait_ge(sem["squares_done"], 2 * j + n + 1)
                v.tensor_tensor(mv[:, 0:count, 1], mv[:, 0:count, 1], sq[:, 0:count],
                                ALU.add).then_inc(sem["sums_done"], 1)

            def group_variance(j, n, count, use):
                dve.wait_ge(sem["sm_ready"], use)
                v.tensor_copy(gs[:, 0:count, :].rearrange("p k t -> p (k t)"),
                              sm[:, 0:2 * count]).then_inc(sem["group_read"], 1)
                dve.wait_ge(sem["group_read"], 2 * j + n + 1)
                v.tensor_tensor(sq[:, 0:count], gs[:, 0:count, 0], gs[:, 0:count, 0],
                                ALU.mult).then_inc(sem["group_square"], 1)
                dve.wait_ge(sem["group_square"], 2 * j + n + 2)
                v.scalar_tensor_tensor(out=var[:, 0:count], in0=gs[:, 0:count, 1], scalar=EPS,
                                       in1=sq[:, 0:count], op0=ALU.add,
                                       op1=ALU.subtract).then_inc(sem["group_var"], 1)

            def y_stats(j, k):
                for h in range(2):
                    dve.wait_ge(sem["y_copied"], 6 * j + 2 * k + h + 1)
                    last = v.bn_stats(st[:, 2 * k + h, :], y[:, k, h * HALF:(h + 1) * HALF])
                if k == 2:
                    last.then_inc(sem["bn_done"], 1)
                    dve.wait_ge(sem["bn_done"], 2 * j + 1)
                    dve.sem_inc(sem["settled_dve"], 1)
                    for k in range(3):
                        last = v.bn_aggr(mv[:, k, :], st[:, 2 * k:2 * k + 2, :].rearrange("p a s -> p (a s)"))
                    last.then_inc(sem["aggr_done"], 1)
                    dve.wait_ge(sem["aggr_done"], 2 * j + 1)
                    group_sums(j, 0, 3)

            def y_coefs(j):
                dve.wait_ge(sem["rstd_done"], 2 * j + 1)
                dve.wait_ge(sem["chosen"], j + 1)
                if not (isinstance(j, int) and j == 0):
                    dve.wait_ge(sem["silu_done"], 3 * j)
                v.tensor_tensor(coef[:, 0, :], rstd[:, :], gb[:, 0, :], ALU.mult).then_inc(sem["coef_scale"], 1)
                dve.wait_ge(sem["coef_scale"], 2 * j + 1)
                v.tensor_tensor(shift[:, :], gs[:, :, 0], coef[:, 0, :], ALU.mult).then_inc(sem["coef_shift"], 1)
                dve.wait_ge(sem["coef_shift"], 2 * j + 1)
                v.tensor_tensor(coef[:, 1, :], gb[:, 1, :], shift[:, :], ALU.subtract).then_inc(sem["coefs_done"], 1)

            def residual(j, part):
                wk = [(route[:, j, k:k + 1] if isinstance(j, int)
                       else route[:, :, :].rearrange("p b t -> p (b t)")[:, bass.ds(4 * j + k, 1)]) for k in range(TOP)]
                if part == 0:
                    dve.wait_ge(sem["silu_done"], 3 * j + 1)
                    if not (isinstance(j, int) and j == 0):
                        dve.wait_ge(sem["xr_saved"], 16 * j)
                        dve.wait_ge(sem["xw_done"], j)
                    v.tensor_tensor(xr[:, :], y[:, 0, :], xin[:, :], ALU.add).then_inc(sem["sum_shared"], 1)
                    return
                if part == 1:
                    dve.wait_ge(sem["silu_done"], 3 * j + 2)
                    dve.wait_ge(sem["sum_shared"], j + 1)
                    v.scalar_tensor_tensor(out=xr[:, :], in0=y[:, 1, :], scalar=wk[0], in1=xr[:, :],
                                           op0=ALU.mult, op1=ALU.add).then_inc(sem["sum_first"], 1)
                    return
                dve.wait_ge(sem["silu_done"], 3 * j + 3)
                dve.wait_ge(sem["sum_first"], j + 1)
                v.scalar_tensor_tensor(out=xr[:, :], in0=y[:, 2, :], scalar=wk[1], in1=xr[:, :],
                                       op0=ALU.mult, op1=ALU.add).then_inc(sem["xr_done"], 1)
                dve.wait_ge(sem["xr_done"], j + 1)
                for h in range(2):
                    last = v.bn_stats(st[:, h, :], xr[:, h * HALF:(h + 1) * HALF])
                last.then_inc(sem["bn_done"], 1)
                dve.wait_ge(sem["bn_done"], 2 * j + 2)
                dve.sem_inc(sem["settled_dve"], 1)
                v.bn_aggr(mv[:, 0, :], st[:, 0:2, :].rearrange("p a s -> p (a s)")).then_inc(sem["aggr_done"], 1)
                dve.wait_ge(sem["aggr_done"], 2 * j + 2)
                group_sums(j, 1, 1)

            def x_coefs(j):
                dve.wait_ge(sem["rstd_done"], 2 * j + 2)
                v.tensor_copy(coef2[:, 0:1], rstd[:, 0:1]).then_inc(sem["coef_scale"], 1)
                v.scalar_tensor_tensor(out=coef2[:, 1:2], in0=gs[:, 0, 0:1], scalar=-1.0, in1=rstd[:, 0:1],
                                       op0=ALU.mult, op1=ALU.mult).then_inc(sem["coef_shift"], 1)

            def maxima(b, p):
                s = PAIRS * b + p
                dve.wait_ge(sem["s_ready"], s + 1)
                v.tensor_reduce(mx[:, :], sbk[p % 2][:, :].rearrange("p (h m) -> p h m", h=HEADS), AX.X,
                                ALU.max).then_inc(sem["s_max"], 1)
                dve.wait_ge(sem["s_max"], s + 1)
                v.tensor_copy(cm[:, 0:HEADS], mx[:, :]).then_inc(sem["c_hi"], 1)
                dve.wait_ge(sem["c_hi"], s + 1)
                v.tensor_tensor(cm[:, HEADS:2 * HEADS], mx[:, :], cm[:, 0:HEADS], ALU.subtract).then_inc(sem["c_lo"], 1)

            def outputs(b, r):
                n = ROWS * b + r
                dve.wait_ge(sem["pv_done"], PAIRS * b + 2 * r + 2)
                v.reciprocal(rec[:, :], pvb[:, WROW:2 * WROW]).then_inc(sem["recip_done"], 1)
                dve.wait_ge(sem["recip_done"], n + 1)
                if r == 0 and not (isinstance(b, int) and b == 0):
                    dve.wait_ge(sem["acc_done"], 2 * b)
                v.tensor_tensor(o[:, r * WROW:(r + 1) * WROW].rearrange("p (r x c) -> p x r c", r=WS, x=ROWS),
                                pvb[:, 0:WROW].rearrange("p (x r c) -> p x r c", r=WS, x=ROWS),
                                rec[:, :].rearrange("p (x r c) -> p x r c", r=WS, x=ROWS),
                                ALU.mult).then_inc(sem["o_done"], 1)

            def low_qk(b, n):
                dst, col, hi, lo = ((qhl, BQ, "q_hi", "q_lo"), (khl, BK, "k_hi", "k_lo"))[n]
                for h in range(2):
                    part = slice(h * HALF, (h + 1) * HALF)
                    dve.wait_ge(sem[hi], 2 * b + h + 1)
                    v.scalar_tensor_tensor(out=dst[:, 1, part], in0=g[h][:, :], scalar=w[:, col:col + 1],
                                           in1=dst[:, 0, part], op0=ALU.add, op1=ALU.subtract
                                           ).then_inc(sem[lo], 1)

            def part_k(b):
                dve.wait_ge(sem["k_lo"], 2 * b + 2)
                dve.wait_ge(sem["k_saved"], 16 * b)
                for t in range(2):
                    for par in range(2):
                        last = v.tensor_scalar(kpar[:, t, :, par, :], khl[:, t, :].rearrange("p (w m) -> p w m", m=TOK),
                                               cc[:, PM + par:PM + par + 1], None, ALU.mult)
                last.then_inc(sem["k_split"], 1)

            def turn_v(b):
                dve.wait_ge(sem["v_done"], 2 * b + 2)
                dve.wait_ge(sem["vt_done"], b)
                v.transpose(vtmp[:, :].rearrange("p (c y) -> p y c", c=QD),
                            vn[:, :].rearrange("p (y x) -> p y x", x=W)[:, :, ::-1]).then_inc(sem["v_turned"], 1)

            def step(b, has1, has2, has3):
                for p in range(PAIRS):
                    s = PAIRS * b + p
                    if has2 and p == P_Y + 1:
                        group_variance(b + 2, 0, 3, sm_use(b, "gn_y"))
                    dve.wait_ge(sem["sm_ready"], sm_use(b, f"max{p}"))
                    dve.wait_ge(sem["st_ready"], s)
                    v.tensor_copy(ct[0:2 * HEADS, :], smb[0:2 * HEADS, 0:C]).then_inc(sem["ct_done"], 1)
                    if p < PAIRS - 1:
                        maxima(b, p + 1)
                    if p % 2 == 0 and p:
                        outputs(b, p // 2 - 1)
                    if has2 and p == TOP + 1:
                        y_stats(b + 2, TOP)
                    if has1 and p in (P_QK, P_QK + 1):
                        low_qk(b + 1, p - P_QK)
                    if has2 and p == P_Y + 1:
                        y_coefs(b + 2)
                    if has2 and p < TOP:
                        y_stats(b + 2, p)
                    if has1 and p == P_QK + 2:
                        part_k(b + 1)
                    if has2 and p in range(P_X, P_X + 3):
                        residual(b + 2, p - P_X)
                outputs(b, ROWS - 1)
                if has1:
                    maxima(b + 1, 0)
                    turn_v(b + 1)
                if has2:
                    group_variance(b + 2, 1, 1, sm_use(b, "gn_x"))
                for h in range(2):
                    dve.wait_ge(sem["proj_ready"], 2 * b + h + 1)
                    dve.wait_ge(sem["x1_loaded"], 16 * b + 16)
                    part = slice(h * HALF, (h + 1) * HALF)
                    v.scalar_tensor_tensor(out=x1[:, part], in0=tbk[h][:, :], scalar=btot[:, 0:1], in1=x1[:, part],
                                           op0=ALU.add, op1=ALU.add).then_inc(sem["acc_done"], 1)
                if has2:
                    x_coefs(b + 2)

            for k in range(3):
                y_stats(0, k)
            group_variance(0, 0, 3, SM_SETUP + 1)
            y_coefs(0)
            residual(0, 0)
            residual(0, 1)
            residual(0, 2)
            group_variance(0, 1, 1, SM_SETUP + 2)
            x_coefs(0)
            low_qk(0, 0)
            low_qk(0, 1)
            part_k(0)
            turn_v(0)
            for k in range(3):
                y_stats(1, k)
            group_variance(1, 0, 3, SM_SETUP + 3)
            y_coefs(1)
            maxima(0, 0)
            residual(1, 0)
            residual(1, 1)
            residual(1, 2)
            group_variance(1, 1, 1, SM_SETUP + 4)
            x_coefs(1)
            images(dve, step)

            for c in range(QD):
                r = c % TAP_RING
                dve.wait_ge(sem["tap_hi"], c + 1)
                v.tensor_tensor(taps16[0:C // 2, r, 1, :], taps[0:C // 2, r, :], taps16[0:C // 2, r, 0, :],
                                ALU.subtract).then_inc(sem["tap_lo"], 1)
                dve.wait_ge(sem["tap_lo"], c + 1)
                v.tensor_copy(taps16[C // 2:C, r, :, :].rearrange("p t n -> p (t n)"),
                              taps16[0:C // 2, r, :, :].rearrange("p t n -> p (t n)")).then_inc(sem["tap_ready"], 1)

            def turn_back(b):
                dve.wait_ge(sem["dw_copied"], QD)
                if b >= 2:
                    dve.wait_ge(sem["g_ready"], LAST_USE + 2 * (b - 1))
                dst = (vn, vtmp)[b % 2][:, :].rearrange("p (i y x) -> p i y x", i=2, x=W)
                for half in range(2):
                    last = v.transpose(dst[:, half], pe_t[:, half, b].rearrange("p c y -> p y c"))
                last.then_inc(sem["pe_turned"], 1)

            turn_back(0)
            dve.wait_ge(sem["acc_loaded"], 16 * B)
            for b in range(B):
                if b + 1 < B:
                    turn_back(b + 1)
                for h in range(2) if b % 2 == 0 else ():
                    dve.wait_ge(sem["g_ready"], LAST_USE + 2 * b + h + 1)
                    part = slice(h * HALF, (h + 1) * HALF)
                    v.tensor_tensor(acc[b][:, part], g[h][:, :], acc[b][:, part], ALU.add).then_inc(sem["out_done"], 1)

        @block.tensor
        def _(pe):
            mm = nc.tensor.matmul
            pe.wait_ge(sem["w_loaded"], 64)
            for n, bk in enumerate((tbk[0], sbk[0])):
                at = TBL + n * TABLE // 2
                last = mm(bk[:, 0:TABLE // 2], l1s[:, :], tc[0:3, at:at + TABLE // 2], start=True, stop=True)
            last.then_inc(sem["setup_pe"], 1)
            pe.wait_ge(sem["setup_act"], 1)
            for m in range(TOK):
                at = (WS - 1 - m % WS) * REL * WS + (WS - 1 - m // WS) * WS
                for part in range(2):
                    last = mm(tbk[1][TOK * part:TOK * part + TOK, HEADS * m:HEADS * m + HEADS],
                              hb[:, at:at + TOK], w[:, CW2:CW2 + HEADS], start=True, stop=True)
            last.then_inc(sem["setup_pe"], 1)
            pe.wait_ge(sem["setup_dve"], 7)
            mm(sm[:, 0:2 * B], cc[:, AV4:AV4 + C], sgs[:, :, :].rearrange("p b t -> p (b t)"), start=True,
               stop=True).then_inc(sem["sm_ready"], 1)
            pe.wait_ge(sem["setup_dve"], 11)
            mm(sm[0:B, 0:E], smv[:, :, 0], w[:, RWM:RWM + E], start=True, stop=False)
            mm(sm[0:B, 0:E], smv[:, :, 1], w[:, RWS:RWS + E], start=False, stop=True).then_inc(sem["sm_ready"], 1)
            pe.wait_ge(sem["setup_dve"], 28)
            mm(sm[:, 0:4 * B], tc[0:B, ONE:ONE + C], rb[:, :, :].rearrange("p b t -> p (b t)"), start=True,
               stop=True).then_inc(sem["sm_ready"], 1)
            pe.wait_ge(sem["setup_read"], 3)
            mm(sm[:, 0:1], w[:, WP:WP + C], w[:, BV:BV + 1], start=True, stop=True).then_inc(sem["sm_ready"], 1)
            pe.wait_ge(sem["setup_dve"], 34)

            def convolve(j, k):
                first = isinstance(j, int) and j == 0
                if k == 0:
                    pe.wait_ge(sem["xn_done"], j + 1)
                    for h in range(2):
                        if isinstance(j, int) and j == 2:
                            pe.wait_ge(sem["y_copied"], G_CONV + 2 * TOP + h + 1)
                        elif isinstance(j, int) and j == 1:
                            pe.wait_ge(sem["vp_done"], 2 * h + 2)
                        elif not first:
                            pe.wait_ge(sem["vp_done"], 4 * (j - 2) + 2 * h + 2)
                        mm(g[h][:, :], w[:, WSH:WSH + C], xn[:, 1 + 16 * h:17 + 16 * h, 1:W + 1], start=True,
                           stop=True).then_inc(sem["g_ready"], 1)
                    return
                if k == 1:
                    pe.wait_ge(sem["rows_loaded"], 32 * TOP * (j + 1))
                    pe.wait_ge(sem["chosen_w"], 16 * TOP * (j + 1))
                for h in range(2):
                    pe.wait_ge(sem["y_copied"], 6 * j + 2 * (k - 1) + h + 1)
                    for dy in range(2):
                        last = mm(g[h][:, :], wsel[:, k - 1, C * dy:C * dy + C],
                                  xsh[:, k - 1, dy + 16 * h:dy + 16 * h + 16, 0:W], start=(dy == 0), stop=(dy == 1))
                    last.then_inc(sem["g_ready"], 1)

            def average(j, n, count, col, maxima=0):
                pe.wait_ge(sem["sums_done"], 2 * j + n + 1)
                if n or not (isinstance(j, int) and j == 0):
                    pe.wait_ge(sem["group_read"], 2 * j + n)
                pe.wait_ge(sem["ct_done"], maxima)
                mm(sm[:, 0:2 * count], cc[:, col:col + C], mv[:, 0:count, :].rearrange("p k t -> p (k t)"),
                   start=True, stop=True).then_inc(sem["sm_ready"], 1)

            def project_qk(b, n):
                if n == 0:
                    pe.wait_ge(sem["xw_done"], b + 1)
                    if isinstance(b, int) and b == B - 1:
                        pe.wait_ge(sem["vp_done"], 4 * (b - 1) + 4)
                    elif isinstance(b, int) and b == 0:
                        pe.wait_ge(sem["y_copied"], G_CONV)
                    else:
                        pe.wait_ge(sem["y_copied"], G_CONV * b + 2 * G_CONV)
                for h in range(2):
                    if n:
                        pe.wait_ge(sem["q_lo"], 2 * b + h + 1)
                    mm(g[h][:, :], w[:, (WQ, WK)[n]:(WQ, WK)[n] + C], xw[:, h * HALF:(h + 1) * HALF], start=True,
                       stop=True).then_inc(sem["g_ready"], 1)

            def project_v(b):
                nat = xw[:, :].rearrange("p (wy wx r c) -> p wy r wx c", wy=ROWS, r=WS, wx=ROWS)
                for h in range(2):
                    pe.wait_ge(sem["k_lo"], 2 * b + h + 1)
                    for k in range(2):
                        last = mm(g[h][:, k * WROW:(k + 1) * WROW], w[:, WV:WV + C], nat[:, 2 * h + k],
                                  start=True, stop=True)
                    last.then_inc(sem["g_ready"], 1)

            def project_vt(b):
                wv = w[:, WV:WV + C].rearrange("p (i t c) -> p t i c", i=Q, t=2)
                for h in range(2):
                    pe.wait_ge(sem["v_done"], 2 * b + h + 1)
                    for n in range(PAIRS):
                        win = PAIRS * h + n
                        for par in range(2):
                            last = mm(g[h][TOK * par:TOK * par + TOK, n * TOK:n * TOK + TOK],
                                      xw[:, win * TOK:win * TOK + TOK], wv[:, par], start=True, stop=True)
                    last.then_inc(sem["g_ready"], 1)

            def scores(b, p):
                s = PAIRS * b + p
                if p == 0:
                    pe.wait_ge(sem["stacked0"], 96 * b + 96)
                if p == PAIRS // 2:
                    pe.wait_ge(sem["stacked1"], 96 * b + 96)
                pe.wait_ge(sem["s_max"], PAIRS * b + max(p - 1, 0))
                bk = sbk[p % 2]
                mm(bk[:, :], ident2[:, :], bias[:, :], start=True, stop=False, skip_group_check=True)
                for i in range(Q):
                    for n in range(2):
                        at = (2 * p + n) * TOK
                        last = mm(bk[TOK * n:TOK * n + TOK, C * i:C * i + C], qs[0:3 * QD, i, at:at + TOK],
                                  ks[0:3 * QD, i, 2 * at:2 * at + C], start=False, stop=(i == Q - 1), skip_group_check=True)
                last.then_inc(sem["s_ready"], 1)

            def turned_scores(b, p):
                pe.wait_ge(sem["exp_done"], PAIRS * b + max(p - 1, 0))
                if p < 2 and not (isinstance(b, int) and b == 0):
                    pe.wait_ge(sem["acc_done"], 2 * b - 1 + p)
                bk = tbk[p % 2][:, :].rearrange("p (w i n) -> p i w n", w=2, i=Q)
                for i in range(Q):
                    mm(bk[:, i], bias[:, C * i:C * i + C], ident2[:, :], start=(i == 0), stop=False,
                       skip_group_check=True)
                for i in range(Q):
                    for n in range(2):
                        at = (2 * p + n) * TOK
                        mm(bk[:, i, n], ks[0:3 * QD, i, 2 * at:2 * at + C], qs[0:3 * QD, i, at:at + TOK],
                           start=False, stop=False, skip_group_check=True)

            def less_maxima(b, p):
                s = PAIRS * b + p
                bk = tbk[p % 2][:, :].rearrange("p (w i n) -> p i w n", w=2, i=Q)
                pe.wait_ge(sem["ct_done"], s + 1)
                for i in range(Q):
                    last = mm(bk[:, i], sel[:, C * i:C * i + C], ct[:, :], start=False, stop=(i == Q - 1),
                              skip_group_check=True)
                last.then_inc(sem["st_ready"], 1)

            def values(b, p):
                s = PAIRS * b + p
                pe.wait_ge(sem["exp_done"], s + 1)
                if p == 0:
                    pe.wait_ge(sem["vp_done"], 4 * b + 4)
                if p % 2 == 0:
                    pe.wait_ge(sem["o_done"], ROWS * b + p // 2)
                at = (p % 2) * 2 * TOK
                for n in range(2):
                    for i in range(Q):
                        mm(pvb[QD * i:QD * i + QD, at + n * TOK:at + n * TOK + TOK], vp[:, 2 * p + n, i, :],
                           pt[:, p % 2, n, i, :], start=True, stop=True)
                for i in range(Q):
                    last = mm(pvb[QD * i:QD * i + QD, WROW + at:WROW + at + 2 * TOK], cc[:, OM:OM + QD],
                              pt[:, p % 2, :, i, :], start=True, stop=True)
                last.then_inc(sem["pv_done"], 1)

            def turn_maxima(b, p, has2):
                pe.wait_ge(sem["c_lo"], PAIRS * b + p + 1)
                pe.wait_ge(sem["ct_done"], PAIRS * b + p)
                pe.wait_ge(sem["group_read"], min(2 * b + 4, 2 * B) if isinstance(b, int) and not has2
                           else 2 * b + 4 + (p > P_Y))
                nc.tensor.transpose(smb[0:2 * HEADS, 0:C], cm[:, :], identb[:, :]).then_inc(sem["sm_ready"], 1)

            def step(b, has1, has2, has3):
                if has2:
                    convolve(b + 2, 0)
                for p in range(PAIRS):
                    if p + 1 < PAIRS:
                        scores(b, p + 1)
                    if has2 and p == P_Y + 1:
                        average(b + 2, 0, 3, AV16, PAIRS * b + p)
                    turn_maxima(b, p, has2)
                    turned_scores(b, p)
                    if p:
                        values(b, p - 1)
                    less_maxima(b, p)
                    if has2 and p < TOP:
                        convolve(b + 2, p + 1)
                    if has1 and p in (P_QK, P_QK + 1):
                        project_qk(b + 1, p - P_QK)
                if has1:
                    project_v(b + 1)
                    scores(b + 1, 0)
                values(b, PAIRS - 1)
                if has2:
                    average(b + 2, 1, 1, AV4, PAIRS * (b + 1))
                if has1:
                    project_vt(b + 1)
                pe.wait_ge(sem["o_done"], ROWS * b + ROWS)
                for h in range(2):
                    mm(tbk[h][:, :], w[:, WP:WP + C], o[:, h * HALF:(h + 1) * HALF], start=True,
                       stop=True).then_inc(sem["proj_ready"], 1)

            for k in range(3):
                convolve(0, k)
            average(0, 0, 3, AV16)
            average(0, 1, 1, AV4)
            project_qk(0, 0)
            project_qk(0, 1)
            project_v(0)
            project_vt(0)
            for k in range(3):
                convolve(1, k)
            scores(0, 0)
            average(1, 0, 3, AV16)
            average(1, 1, 1, AV4)
            images(pe, step)

            for c in range(QD):
                pe.wait_ge(sem["tap_ready"], c + 1)
                if c >= 4:
                    pe.wait_ge(sem["dw_copied"], c - 3)
                elif c == 0:
                    pe.wait_ge(sem["vt_saved"], 64 * B)
                elif c == 2:
                    pe.wait_ge(sem["acc_done"], 2 * B)
                bk = (sbk + tbk)[c % 4]
                tap = taps16[:, c % TAP_RING, :, :].rearrange("p t (i d m) -> p t i d m", i=2, d=DWK)
                for dy in range(DWK):
                    for t in range(2):
                        for i in range(2):
                            last = mm(bk[C // 2 * i:C // 2 * (i + 1), :], tap[:, t, i, dy, :],
                                      vt16[:, i, :, c, dy:dy + H], start=(dy == 0 and t == 0),
                                      stop=(dy == DWK - 1 and t == 1))
                last.then_inc(sem["dw_ready"], 1)
            for b in range(B):
                pe.wait_ge(sem["pe_turned"], b + 1)
                for h in range(2):
                    if b:
                        pe.wait_ge(sem["out_done" if b % 2 else "evac_done"], 2 * ((b - 1) // 2) + h + 1)
                    else:
                        pe.wait_ge(sem["acc_done"], 2 * (B - 1) + h + 1)
                    mm(g[h][:, :], w[:, WP:WP + C], (vn, vtmp)[b % 2][:, h * HALF:(h + 1) * HALF], start=True,
                       stop=True).then_inc(sem["g_ready"], 1)


def _lay_out(np, a):
    f = np.float32
    g = C // HEADS
    t = np.ascontiguousarray
    qkv = a["L1_conv_qkv_w"]
    shared = np.zeros((C, C), f)
    for n in range(HEADS):
        r = slice(g * n, g * n + g)
        shared[r, r] = a["L0_conv_shared_w"][r, :, 0, 0].T
    rw = a["L0_conv_router_w"]
    cols = [qkv[0:C].T, qkv[C:2 * C].T, qkv[2 * C:].T, a["L1_conv_proj_w"].T, shared, rw[:, 0:C].T, rw[:, C:].T,
            a["L1_conv_cpb_w2"].T, a["L0_conv_expert_g"].T, a["L0_conv_expert_b"].T]
    cols += [v.reshape(C, 1) for v in (a["L0_conv_gn_shared_g"], a["L0_conv_gn_shared_b"], a["L1_conv_qkv_b"][0:C],
                                      a["L1_conv_qkv_b"][C:2 * C], a["L1_conv_qkv_b"][2 * C:], a["L1_conv_proj_b"])]
    wa = t(np.concatenate(cols, axis=1))
    fused = a["L0_conv_fused_w"].reshape(E, C, GC, 3, 3).transpose(0, 3, 4, 2, 1)
    wx = np.zeros((E, 2, 3, GC, 2, C), f)
    wx[:, :, :, :, 0] = fused[:, 0:2]
    wx[:, 1, :, :, 1] = fused[:, 2]
    wx = wx.reshape(E, SH, 2 * C)
    dw = np.zeros((2, QD, 2, DWK, HANK), f)
    dw[:, :, :, :, W - 1 - PAD:W + PAD] = a["L1_conv_dw_w"][:, 0, :, ::-1].reshape(2, 2, QD, DWK, DWK).transpose(1, 2, 0, 3, 4)
    l1 = t(np.concatenate([a["L1_conv_cpb_w1"].T, a["L1_conv_cpb_b1"].reshape(1, C)], axis=0))
    n = np.arange(C)
    cst = np.zeros((C, CCOLS), f)
    cst[:, AV4:AV4 + C] = (n[:, None] // 4 == n[None] // 4) * 0.25
    cst[:, AV16:AV16 + C] = (n[:, None] // 16 == n[None] // 16) * 0.0625
    cst[:, OM:OM + QD] = n[:, None] // TOK == np.arange(QD)[None] // HD
    cst[:, PM:PM + 2] = n[:, None] // HD % 2 == np.arange(2)[None]
    tmp = np.zeros((C, TCOLS), f)
    tmp[:, ID:ID + C] = np.eye(C)
    tmp[:, ID2:ID2 + C] = n[:, None] % TOK == n[None] % TOK
    for r in range(2 * HEADS):
        i, par = (r % HEADS) // 2, r % 2
        tmp[r, SEL + C * i + TOK * par:SEL + C * i + TOK * par + TOK] = -1.0
    tmp[0:B, EYE:EYE + B] = np.eye(B)
    tmp[0:B, ONE:ONE + C] = 1.0
    r = np.arange(-(WS - 1), WS, dtype=f)
    grid = np.stack(np.meshgrid(r, r, indexing="ij"), axis=-1) / (WS - 1) * 8.0
    grid = (np.sign(grid) * np.log2(np.abs(grid) + 1.0) / np.log2(8.0)).astype(f).reshape(-1, 2)
    k = np.arange(TABLE)
    tmp[0:2, TBL:] = grid.T[:, (k // WS % REL) * REL + k // (WS * REL) + k % WS]
    tmp[2, TBL:] = 1.0
    return {"wa": wa, "wx": wx, "dw": dw, "l1": l1, "cst": cst, "tmp": tmp}


def kernel(**inputs):
    import numpy as np
    import concourse.bacc as bacc
    from concourse.bass_utils import run_bass_kernel_spmd as run

    arrays = {"x": np.ascontiguousarray(inputs["x"])}
    arrays.update(_lay_out(np, {k: np.asarray(v) for k, v in inputs.items()}))
    nc = bacc.Bacc("TRN2", target_bir_lowering=False, num_devices=1)
    args = {k: nc.dram_tensor(k, v.shape, mybir.dt.from_np(v.dtype), kind="ExternalInput").ap()
            for k, v in arrays.items()}
    out = nc.dram_tensor("out", (B, C, H, W), F32, kind="ExternalOutput").ap()
    program(nc, args["x"], args["wa"], args["wx"], args["dw"], args["l1"], args["cst"], args["tmp"], out)
    r = run(nc, [arrays], core_ids=[0])
    return r.results[0]["out"]
```
